# Optimizing a Trainium2 kernel written in Bass

```python
import numpy as np
import jax
import jax.numpy as jnp

def _softmax(x, axis=-1):
    return jax.nn.softmax(x, axis=axis)

def _gelu(x):
    return jax.nn.gelu(x, approximate=True)

def _silu(x):
    return jax.nn.silu(x)

def _sigmoid(x):
    return jax.nn.sigmoid(x)

def _layernorm(x, axis=-1, eps=1e-05):
    m = jnp.mean(x, axis=axis, keepdims=True)
    v = jnp.var(x, axis=axis, keepdims=True)
    return (x - m) / jnp.sqrt(v + eps)

def _scatter_add(tgt, idx, src, axis=0):
    return tgt.at[idx].add(src)

def _segment_sum(src, seg, n):
    return jax.ops.segment_sum(src, seg, n)
kernel_name = 'mk_dlrm_tower_d1_rec_r8_2c91ea'

def setup_inputs(seed: int=0):
    np.random.seed(seed)
    _w = jnp.asarray

    def _rec_inputs():
        import jax
        import jax.numpy as jnp
        _tk = jax.random.key(seed)
        dense_ctx = jax.random.normal(jax.random.fold_in(_tk, 190), (1024, 16), jnp.float32)
        ids = jnp.stack([jax.random.randint(jax.random.fold_in(_tk, 200 + f), (1024,), 0, v, jnp.int32) for f, v in enumerate([1250, 125000, 1000, 125000, 1000, 12500, 1250, 1000, 1000, 125000, 1000, 1000, 1250, 125000, 1000, 12500, 125000, 1000, 1250, 125000, 12500, 1000, 1250, 12500, 12500, 125000, 1000, 1000, 1000, 1250, 12500, 12500])], axis=1)
        tbl_0 = 0.05 * jax.random.normal(jax.random.fold_in(_tk, 500 + 0), (1250, 16), jnp.float32)
        tbl_1 = 0.05 * jax.random.normal(jax.random.fold_in(_tk, 500 + 1), (125000, 16), jnp.float32)
        tbl_2 = 0.05 * jax.random.normal(jax.random.fold_in(_tk, 500 + 2), (1000, 16), jnp.float32)
        tbl_3 = 0.05 * jax.random.normal(jax.random.fold_in(_tk, 500 + 3), (125000, 16), jnp.float32)
        tbl_4 = 0.05 * jax.random.normal(jax.random.fold_in(_tk, 500 + 4), (1000, 16), jnp.float32)
        tbl_5 = 0.05 * jax.random.normal(jax.random.fold_in(_tk, 500 + 5), (12500, 16), jnp.float32)
        tbl_6 = 0.05 * jax.random.normal(jax.random.fold_in(_tk, 500 + 6), (1250, 16), jnp.float32)
        tbl_7 = 0.05 * jax.random.normal(jax.random.fold_in(_tk, 500 + 7), (1000, 16), jnp.float32)
        tbl_8 = 0.05 * jax.random.normal(jax.random.fold_in(_tk, 500 + 8), (1000, 16), jnp.float32)
        tbl_9 = 0.05 * jax.random.normal(jax.random.fold_in(_tk, 500 + 9), (125000, 16), jnp.float32)
        tbl_10 = 0.05 * jax.random.normal(jax.random.fold_in(_tk, 500 + 10), (1000, 16), jnp.float32)
        tbl_11 = 0.05 * jax.random.normal(jax.random.fold_in(_tk, 500 + 11), (1000, 16), jnp.float32)
        tbl_12 = 0.05 * jax.random.normal(jax.random.fold_in(_tk, 500 + 12), (1250, 16), jnp.float32)
        tbl_13 = 0.05 * jax.random.normal(jax.random.fold_in(_tk, 500 + 13), (125000, 16), jnp.float32)
        tbl_14 = 0.05 * jax.random.normal(jax.random.fold_in(_tk, 500 + 14), (1000, 16), jnp.float32)
        tbl_15 = 0.05 * jax.random.normal(jax.random.fold_in(_tk, 500 + 15), (12500, 16), jnp.float32)
        tbl_16 = 0.05 * jax.random.normal(jax.random.fold_in(_tk, 500 + 16), (125000, 16), jnp.float32)
        tbl_17 = 0.05 * jax.random.normal(jax.random.fold_in(_tk, 500 + 17), (1000, 16), jnp.float32)
        tbl_18 = 0.05 * jax.random.normal(jax.random.fold_in(_tk, 500 + 18), (1250, 16), jnp.float32)
        tbl_19 = 0.05 * jax.random.normal(jax.random.fold_in(_tk, 500 + 19), (125000, 16), jnp.float32)
        tbl_20 = 0.05 * jax.random.normal(jax.random.fold_in(_tk, 500 + 20), (12500, 16), jnp.float32)
        tbl_21 = 0.05 * jax.random.normal(jax.random.fold_in(_tk, 500 + 21), (1000, 16), jnp.float32)
        tbl_22 = 0.05 * jax.random.normal(jax.random.fold_in(_tk, 500 + 22), (1250, 16), jnp.float32)
        tbl_23 = 0.05 * jax.random.normal(jax.random.fold_in(_tk, 500 + 23), (12500, 16), jnp.float32)
        tbl_24 = 0.05 * jax.random.normal(jax.random.fold_in(_tk, 500 + 24), (12500, 16), jnp.float32)
        tbl_25 = 0.05 * jax.random.normal(jax.random.fold_in(_tk, 500 + 25), (125000, 16), jnp.float32)
        tbl_26 = 0.05 * jax.random.normal(jax.random.fold_in(_tk, 500 + 26), (1000, 16), jnp.float32)
        tbl_27 = 0.05 * jax.random.normal(jax.random.fold_in(_tk, 500 + 27), (1000, 16), jnp.float32)
        tbl_28 = 0.05 * jax.random.normal(jax.random.fold_in(_tk, 500 + 28), (1000, 16), jnp.float32)
        tbl_29 = 0.05 * jax.random.normal(jax.random.fold_in(_tk, 500 + 29), (1250, 16), jnp.float32)
        tbl_30 = 0.05 * jax.random.normal(jax.random.fold_in(_tk, 500 + 30), (12500, 16), jnp.float32)
        tbl_31 = 0.05 * jax.random.normal(jax.random.fold_in(_tk, 500 + 31), (12500, 16), jnp.float32)
        _rk = jax.random.fold_in(_tk, 7)
        W_top1 = 0.0693375 * jax.random.normal(jax.random.fold_in(_tk, 801), (208, 512), jnp.float32)
        W_top2 = 0.0441942 * jax.random.normal(jax.random.fold_in(_tk, 802), (512, 256), jnp.float32)
        W_top3 = 0.0625 * jax.random.normal(jax.random.fold_in(_tk, 803), (256, 1), jnp.float32)
        b_top1 = jnp.zeros((512,), jnp.float32)
        b_top2 = jnp.zeros((256,), jnp.float32)
        return (dense_ctx, ids, tbl_0, tbl_1, tbl_2, tbl_3, tbl_4, tbl_5, tbl_6, tbl_7, tbl_8, tbl_9, tbl_10, tbl_11, tbl_12, tbl_13, tbl_14, tbl_15, tbl_16, tbl_17, tbl_18, tbl_19, tbl_20, tbl_21, tbl_22, tbl_23, tbl_24, tbl_25, tbl_26, tbl_27, tbl_28, tbl_29, tbl_30, tbl_31, W_top1, b_top1, W_top2, b_top2, W_top3)
    dense_ctx, ids, tbl_0, tbl_1, tbl_2, tbl_3, tbl_4, tbl_5, tbl_6, tbl_7, tbl_8, tbl_9, tbl_10, tbl_11, tbl_12, tbl_13, tbl_14, tbl_15, tbl_16, tbl_17, tbl_18, tbl_19, tbl_20, tbl_21, tbl_22, tbl_23, tbl_24, tbl_25, tbl_26, tbl_27, tbl_28, tbl_29, tbl_30, tbl_31, W_top1, b_top1, W_top2, b_top2, W_top3 = _rec_inputs()

    def _L0_rec_setup():
        import jax, jax.numpy as jnp
        import numpy as np
        B, M, D = (2048, 32, 16)
        LAYERS = [64, 64, 64]
        key = jax.random.key(seed)
        ks = jax.random.split(key, 4)
        inp = {'embeddings': jax.random.normal(ks[0], (B, M, D), dtype=jnp.float32)}
        hk_1 = M
        for i, hk in enumerate(LAYERS):
            scale = (2.0 / (M * hk_1 + hk)) ** 0.5
            inp[f'W{i}'] = jax.random.normal(ks[i + 1], (M, hk_1, hk), dtype=jnp.float32) * scale
            hk_1 = hk
        return inp
    _L0_rec_all = _L0_rec_setup()
    _L0_rec_in = {k: v for k, v in _L0_rec_all.items() if k in ('W0', 'W1', 'W2')}
    del _L0_rec_all
    return {'dense_ctx': dense_ctx, 'ids': ids, 'tbl_0': tbl_0, 'tbl_1': tbl_1, 'tbl_2': tbl_2, 'tbl_3': tbl_3, 'tbl_4': tbl_4, 'tbl_5': tbl_5, 'tbl_6': tbl_6, 'tbl_7': tbl_7, 'tbl_8': tbl_8, 'tbl_9': tbl_9, 'tbl_10': tbl_10, 'tbl_11': tbl_11, 'tbl_12': tbl_12, 'tbl_13': tbl_13, 'tbl_14': tbl_14, 'tbl_15': tbl_15, 'tbl_16': tbl_16, 'tbl_17': tbl_17, 'tbl_18': tbl_18, 'tbl_19': tbl_19, 'tbl_20': tbl_20, 'tbl_21': tbl_21, 'tbl_22': tbl_22, 'tbl_23': tbl_23, 'tbl_24': tbl_24, 'tbl_25': tbl_25, 'tbl_26': tbl_26, 'tbl_27': tbl_27, 'tbl_28': tbl_28, 'tbl_29': tbl_29, 'tbl_30': tbl_30, 'tbl_31': tbl_31, 'W_top1': W_top1, 'b_top1': b_top1, 'W_top2': W_top2, 'b_top2': b_top2, 'W_top3': W_top3, 'L0_rec_W0': _L0_rec_in['W0'], 'L0_rec_W1': _L0_rec_in['W1'], 'L0_rec_W2': _L0_rec_in['W2']}

def reference(dense_ctx, ids, tbl_0, tbl_1, tbl_2, tbl_3, tbl_4, tbl_5, tbl_6, tbl_7, tbl_8, tbl_9, tbl_10, tbl_11, tbl_12, tbl_13, tbl_14, tbl_15, tbl_16, tbl_17, tbl_18, tbl_19, tbl_20, tbl_21, tbl_22, tbl_23, tbl_24, tbl_25, tbl_26, tbl_27, tbl_28, tbl_29, tbl_30, tbl_31, W_top1, b_top1, W_top2, b_top2, W_top3, L0_rec_W0, L0_rec_W1, L0_rec_W2):
    import jax
    import jax.numpy as jnp

    def _L0_rec_ref(embeddings, W0, W1, W2):
        import jax, jax.numpy as jnp
        import numpy as np
        B, M, D = (2048, 32, 16)
        LAYERS = [64, 64, 64]
        x0 = embeddings
        xk = x0
        outs = []
        for W in (W0, W1, W2):
            xk = jax.nn.relu(jnp.einsum('bmd,bhd,mhk->bkd', x0, xk, W))
            outs.append(jnp.sum(xk, axis=2))
        return jnp.concatenate(outs, axis=1)
    e = jnp.stack([tbl_0[ids[:, 0]], tbl_1[ids[:, 1]], tbl_2[ids[:, 2]], tbl_3[ids[:, 3]], tbl_4[ids[:, 4]], tbl_5[ids[:, 5]], tbl_6[ids[:, 6]], tbl_7[ids[:, 7]], tbl_8[ids[:, 8]], tbl_9[ids[:, 9]], tbl_10[ids[:, 10]], tbl_11[ids[:, 11]], tbl_12[ids[:, 12]], tbl_13[ids[:, 13]], tbl_14[ids[:, 14]], tbl_15[ids[:, 15]], tbl_16[ids[:, 16]], tbl_17[ids[:, 17]], tbl_18[ids[:, 18]], tbl_19[ids[:, 19]], tbl_20[ids[:, 20]], tbl_21[ids[:, 21]], tbl_22[ids[:, 22]], tbl_23[ids[:, 23]], tbl_24[ids[:, 24]], tbl_25[ids[:, 25]], tbl_26[ids[:, 26]], tbl_27[ids[:, 27]], tbl_28[ids[:, 28]], tbl_29[ids[:, 29]], tbl_30[ids[:, 30]], tbl_31[ids[:, 31]]], axis=1)
    z = _L0_rec_ref(e, L0_rec_W0, L0_rec_W1, L0_rec_W2)
    z = z.reshape(z.shape[0], -1)
    h = jnp.concatenate([z, dense_ctx], axis=1)
    h = jnp.maximum(h @ W_top1 + b_top1, 0.0)
    h = jnp.maximum(h @ W_top2 + b_top2, 0.0)
    y = h @ W_top3
    return y

_drawn_inputs = setup_inputs


def setup_inputs(seed=0):
    import zlib

    import numpy as np

    out = dict(_drawn_inputs(seed))
    spreads = {'b_top1': (0.0, 2.0), 'b_top2': (0.0, 0.8)}
    factors = {'tbl_0': 8.0,
     'tbl_1': 8.0,
     'tbl_2': 8.0,
     'tbl_3': 8.0,
     'tbl_4': 8.0,
     'tbl_5': 8.0,
     'tbl_6': 8.0,
     'tbl_7': 8.0,
     'tbl_8': 8.0,
     'tbl_9': 8.0,
     'tbl_10': 8.0,
     'tbl_11': 8.0,
     'tbl_12': 8.0,
     'tbl_13': 8.0,
     'tbl_14': 8.0,
     'tbl_15': 8.0,
     'tbl_16': 8.0,
     'tbl_17': 8.0,
     'tbl_18': 8.0,
     'tbl_19': 8.0,
     'tbl_20': 8.0,
     'tbl_21': 8.0,
     'tbl_22': 8.0,
     'tbl_23': 8.0,
     'tbl_24': 8.0,
     'tbl_25': 8.0,
     'tbl_26': 8.0,
     'tbl_27': 8.0,
     'tbl_28': 8.0,
     'tbl_29': 8.0,
     'tbl_30': 8.0,
     'tbl_31': 8.0,
     'L0_rec_W0': 3.688,
     'L0_rec_W1': 8.0,
     'L0_rec_W2': 8.0,
     'dense_ctx': 7.483}
    for name, (base, spread) in spreads.items():
        noise = np.random.default_rng([zlib.crc32(name.encode()), seed]).standard_normal(out[name].shape)
        drawn = base * np.exp(spread * noise) if base else spread * noise
        out[name] = jnp.asarray(drawn.astype(out[name].dtype))
    for name, factor in factors.items():
        out[name] = (out[name] * factor).astype(out[name].dtype)
    return out
```

```python
import concourse.bass as bass
from concourse import mybir
from contextlib import ExitStack


def cin_tower_kernel(nc, dense_ctx, ids, tables, w_top1, b_top1, w_top2, b_top2, w_top3,
                     w_cin0, w_cin1, w_cin2, y_out):
    fp32, bf16, i32 = mybir.dt.float32, mybir.dt.bfloat16, mybir.dt.int32
    ALU, ACT = mybir.AluOpType, mybir.ActivationFunctionType

    P = 128
    BATCH, FIELDS = ids.shape
    EMB = tables[0].shape[1]
    HID = w_cin1.shape[2]
    CTX = dense_ctx.shape[1]
    TOP1, TOP2 = w_top1.shape[1], w_top2.shape[1]

    BT = P
    TILES = BATCH // BT
    PAR = 2
    HALF = 512
    N = 2 * HALF
    DQ = HALF // BT
    ND = N // BT
    PARTS = 3
    SK = PARTS * FIELDS

    ROWS = FIELDS * HID // P
    ROTS = 5
    RQ = P // FIELDS
    NROT = ROTS * RQ
    SYM = FIELDS - NROT

    A0, B0, C0 = 0, ROWS, ROWS + ROTS
    STEPS = 2 * ROWS + ROTS
    RING = 4

    EARLY = 11
    JOBS = [[] for _ in range(STEPS)]
    for k in range(ROWS - EARLY):
        JOBS[A0 + k].append(("row", EARLY + k))
    JOBS[A0 + 6].append(("stack", 0))
    for k in range(1 + ROTS):
        JOBS[A0 + 8 + k].append(("rot", k))
    for t in range(EARLY):
        JOBS[C0 + (3 * t) // 2].append(("row", t))
    PER_PERIOD = ROWS + 1 + 1 + ROTS
    FIRST_JOBS = [("stack", 0)] + [("rot", k) for k in range(1 + ROTS)] + [("row", t) for t in range(EARLY)]

    TOWER_AT = {7: 0, 17: 1, 20: 2, 23: 3}

    def step_no(p, s, last=False):
        return p * STEPS + ROTS + s - (ROTS if last and s >= C0 else 0)

    def job_no(p, j):
        return p * PER_PERIOD + len(FIRST_JOBS) + j

    STACK_JOB, ROT_JOB, ROW_JOB = ROWS - EARLY, ROWS - EARLY + 1, ROWS - EARLY + 2 + ROTS

    def row_job(p, t):
        return job_no(p - 1, ROW_JOB + t) if t < EARLY else job_no(p, t - EARLY)

    def wait_for(eng, sem, value):
        if isinstance(value, int) and value <= 0:
            return
        eng.wait_ge(sem, value)

    with ExitStack() as ctx:
        def sb(name, shape, dt=fp32):
            return ctx.enter_context(nc.sbuf_tensor(name, shape, dt))

        def sem(name):
            return ctx.enter_context(nc.semaphore(name))

        w0 = sb("w0", [P, ROTS, HID])
        w0_mirror = sb("w0_mirror", [P, ROTS, HID])
        w1 = sb("w1", [P, ROWS, HID])
        w2 = sb("w2", [P, ROWS, HID])
        t1a = sb("t1a", [P, TOP1])
        t1b = sb("t1b", [HID + CTX, TOP1])
        t2 = sb("t2", [P, TOP1 // P, TOP2])
        t3 = sb("t3", [P, TOP2 // P])
        b1 = sb("b1", [P, TOP1 // P])
        b2 = sb("b2", [P, TOP2 // P])
        ident = sb("ident", [P, P])
        ident_h = sb("ident_h", [P, P], bf16)
        fold = sb("fold", [SK, FIELDS])
        unit = sb("unit", [SK, 2 * FIELDS], bf16)
        sel_row = sb("sel_row", [SK, ROWS, P], bf16)
        sel_rot = sb("sel_rot", [SK, 1 + ROTS, P], bf16)
        idx = sb("idx", [P, FIELDS], i32)
        emb = sb("emb", [P, FIELDS * EMB])
        zero = sb("zero", [P, 1])
        rest = sb("rest", [P, FIELDS * EMB])
        parts = sb("parts", [P, PARTS, FIELDS * EMB], bf16)
        dense = sb("dense", [P, CTX])
        stack = sb("stack", [SK, N], bf16)
        rows = sb("rows", [P, ROWS, N])
        rots = sb("rots", [P, 1 + ROTS, N])
        prod = sb("prod", [P, RING + 1, N])
        x1 = sb("x1", [P, N])
        x2 = sb("x2", [P, N])
        x3 = sb("x3", [HID, N])
        tmp = [sb(f"tmp{n}", [P, HALF + HALF // 2]) for n in range(1, 4)]
        half_sum = sb("half_sum", [P, 3, BT])
        za = sb("za", [P, BT])
        zb = sb("zb", [HID + CTX, BT])
        h1 = sb("h1", [P, TOP1 // P, BT])
        h2 = sb("h2", [P, TOP2 // P, BT])
        yv = sb("yv", [1, BT])

        spread = [ctx.enter_context(nc.psum_tensor(f"spread{i}", [P, N], fp32)) for i in range(2)]
        acc0 = ctx.enter_context(nc.psum_tensor("acc0", [P, HALF], fp32))
        acc1 = ctx.enter_context(nc.psum_tensor("acc1", [P, HALF], fp32))
        acc2 = ctx.enter_context(nc.psum_tensor("acc2", [P, HALF], fp32))
        tower = ctx.enter_context(nc.psum_tensor("tower", [P, HALF], fp32))

        w0_wide = nc.dram_tensor("w0_wide", [FIELDS, 2 * FIELDS, HID], fp32, kind="Internal").ap()
        w0_tall = nc.dram_tensor("w0_tall", [2 * FIELDS, FIELDS, HID], fp32, kind="Internal").ap()

        s_wide = sem("s_wide")
        s_w0 = sem("s_w0")
        s_w12 = sem("s_w12")
        s_top = sem("s_top")
        s_idx = sem("s_idx")
        s_dense = sem("s_dense")
        s_ident0 = sem("s_ident0")
        s_ident = sem("s_ident")
        s_const = sem("s_const")
        s_sel = sem("s_sel")
        s_w0sum = sem("s_w0sum")
        s_gather = sem("s_gather")
        s_split = sem("s_split")
        s_add = [sem(f"s_add{n}") for n in range(1, 4)]
        s_parts = sem("s_parts")
        s_spread = sem("s_spread")
        s_copied = sem("s_copied")
        s_prod = sem("s_prod")
        s_used = sem("s_used")
        s_x1 = sem("s_x1")
        s_x2 = sem("s_x2")
        s_x3 = sem("s_x3")
        s_sum1 = sem("s_sum1")
        s_sum2 = sem("s_sum2")
        s_sum3 = sem("s_sum3")
        s_tower = sem("s_tower")
        s_act = sem("s_act")
        s_y = sem("s_y")

        block = ctx.enter_context(nc.Block())

        @block.sync
        def _(sp):
            def load_tile(i):
                if not (isinstance(i, int) and i == 0):
                    sp.wait_ge(s_gather, i * FIELDS * 16)
                sp.dma_start(idx[:, :], ids[bass.ts(i, BT), :]).then_inc(s_idx, 16)

            def load_dense(i):
                if not (isinstance(i, int) and i == 0):
                    sp.wait_ge(s_tower, (i - 1) * 4 + 1)
                sp.dma_start(dense[:, :], dense_ctx[bass.ts(i, BT), :]).then_inc(s_dense, 16)

            def store(i):
                sp.wait_ge(s_act, (i + 1) * 4)
                sp.dma_start(y_out[bass.ts(i, BT), :].rearrange("b o -> o b"), yv[:, :]).then_inc(s_y, 16)
                sp.wait_ge(s_y, (i + 1) * 16)

            load_tile(0)
            for c in range(2):
                sp.dma_start(w0_wide[:, c * FIELDS:(c + 1) * FIELDS, :], w_cin0).then_inc(s_wide, 16)
                sp.dma_start(w0_tall[c * FIELDS:(c + 1) * FIELDS, :, :], w_cin0).then_inc(s_wide, 16)
            load_dense(0)
            sp.dma_start(w1[:, :, :], w_cin1.rearrange("m h k -> (m h) k").rearrange("(t p) k -> p t k", p=P)).then_inc(s_w12, 16)
            sp.dma_start(w2[:, :, :], w_cin2.rearrange("m h k -> (m h) k").rearrange("(t p) k -> p t k", p=P)).then_inc(s_w12, 16)
            sp.wait_ge(s_wide, 64)
            for q in range(RQ):
                at = slice(q * FIELDS, (q + 1) * FIELDS)
                sp.dma_start(w0[at, :, :], bass.AP(w0_wide.tensor, q * HID, [
                    [(2 * FIELDS + 1) * HID, FIELDS], [RQ * HID, ROTS], [1, HID]])).then_inc(s_w0, 16)
                sp.dma_start(w0_mirror[at, :, :], bass.AP(w0_tall.tensor, q * FIELDS * HID, [
                    [(FIELDS + 1) * HID, FIELDS], [RQ * FIELDS * HID, ROTS], [1, HID]])).then_inc(s_w0, 16)
            sp.dma_start(t1a[:, :], w_top1[0:P, :]).then_inc(s_top, 16)
            sp.dma_start(t1b[:, :], w_top1[P:, :]).then_inc(s_top, 16)
            sp.dma_start(t2[:, :, :], w_top2.rearrange("(t p) n -> p t n", p=P)).then_inc(s_top, 16)
            sp.dma_start(t3[:, :], w_top3.rearrange("(t p) o -> p (t o)", p=P),
                         allow_slow_non_contiguous=True).then_inc(s_top, 16)
            sp.dma_start(b1[:, :], b_top1.rearrange("(t p) -> p t", p=P),
                         allow_slow_non_contiguous=True).then_inc(s_top, 16)
            sp.dma_start(b2[:, :], b_top2.rearrange("(t p) -> p t", p=P),
                         allow_slow_non_contiguous=True).then_inc(s_top, 16)
            load_tile(1)
            with sp.Fori(1, TILES - 1) as i:
                load_tile(i + 1)
                store(i - 1)
                load_dense(i)
            store(TILES - 2)
            load_dense(TILES - 1)
            store(TILES - 1)

        @block.gpsimd
        def _(pool):
            nc.gpsimd.memset(zero[:, :], 0.0).then_inc(s_ident0, 1)
            zeros = zero[:, :].to_broadcast([P, FIELDS * EMB])
            nc.gpsimd.memset(ident[:, :], 0.0).then_inc(s_ident0, 1)
            pool.wait_ge(s_ident0, 2)
            nc.gpsimd.affine_select(out=ident[:, :], in_=ident[:, :], compare_op=ALU.not_equal, fill=1.0,
                                    base=0, pattern=[[-1, P]], channel_multiplier=1).then_inc(s_ident, 1)

            def gather(i):
                pool.drain()
                for f in range(FIELDS):
                    pool.indirect_dma_start(
                        out=emb[:, f * EMB:(f + 1) * EMB], out_offset=None, in_=tables[f],
                        in_offset=bass.IndirectOffsetOnAxis(ap=idx[:, f:f + 1], axis=0)).then_inc(s_gather, 16)

            def split(i):
                pool.drain()
                nc.gpsimd.tensor_tensor(parts[:, 0, :], emb[:, :], zeros, ALU.add).then_inc(s_split, 1)
                pool.wait_ge(s_split, i * 3 + 1)
                nc.gpsimd.tensor_tensor(rest[:, :], emb[:, :], parts[:, 0, :], ALU.subtract).then_inc(s_split, 1)
                pool.wait_ge(s_split, i * 3 + 2)
                nc.gpsimd.tensor_tensor(parts[:, 1, :], rest[:, :], zeros, ALU.add).then_inc(s_split, 1)
                pool.wait_ge(s_split, i * 3 + 3)
                nc.gpsimd.tensor_tensor(parts[:, 2, :], rest[:, :], parts[:, 1, :], ALU.subtract).then_inc(s_parts, 1)

            def sum_d(x, lo, layer, i, par, out, done):
                r = slice(lo, lo + HID)
                q = HALF // 2
                add, base = s_add[layer], i * 5 + 2 * par
                t = tmp[layer]
                nc.gpsimd.tensor_tensor(t[r, 0:HALF], x[r, 0:HALF], x[r, HALF:N], ALU.add).then_inc(add, 1)
                pool.wait_ge(add, base + 1)
                nc.gpsimd.tensor_tensor(t[r, HALF:HALF + q], t[r, 0:q], t[r, q:HALF], ALU.add).then_inc(add, 1)
                pool.wait_ge(add, base + 2)
                a, b = t[r, HALF:HALF + BT], t[r, HALF + BT:HALF + q]
                if par == 0:
                    nc.gpsimd.tensor_tensor(half_sum[r, layer, :], a, b, ALU.add).then_inc(done, 1)
                else:
                    nc.gpsimd.tensor_tensor(t[r, 0:BT], a, b, ALU.add).then_inc(add, 1)
                    pool.wait_ge(add, base + 3)
                    nc.gpsimd.tensor_tensor(out, t[r, 0:BT], half_sum[r, layer, :], ALU.add).then_inc(done, 1)

            def sum1(i, par, *also):
                pool.drain()
                for sem_, value in also:
                    pool.wait_ge(sem_, value)
                pool.wait_ge(s_x1, i * PAR + par + 1)
                sum_d(x1, 0, 0, i, par, za[0:HID, :], s_sum1)

            def sum2(i, par, *also):
                pool.drain()
                for sem_, value in also:
                    pool.wait_ge(sem_, value)
                pool.wait_ge(s_x2, i * PAR + par + 1)
                sum_d(x2, HID, 1, i, par, za[HID:P, :], s_sum2)

            def sum3(i, par, *also):
                pool.drain()
                for sem_, value in also:
                    pool.wait_ge(sem_, value)
                pool.wait_ge(s_x3, i * PAR + par + 1)
                sum_d(x3, 0, 2, i, par, zb[0:HID, :], s_sum3)

            def turn(i, first=False, last=False):
                if not first:
                    sum3(i - 1, 1)
                if last:
                    sum1(i, 0)
                else:
                    sum1(i, 0, (s_idx, (i + 2) * 16))
                if not last:
                    gather(i + 1)
                    sum2(i, 0, (s_gather, (i + 2) * FIELDS * 16))
                    split(i + 1)
                else:
                    sum2(i, 0)
                sum3(i, 0)
                sum1(i, 1)
                sum2(i, 1)

            pool.wait_ge(s_idx, 16)
            gather(0)
            pool.wait_ge(s_gather, FIELDS * 16)
            split(0)
            turn(0, first=True)
            with pool.Fori(1, TILES - 1) as i:
                turn(i)
            turn(TILES - 1, last=True)
            sum3(TILES - 1, 1)

        @block.vector
        def _(dve):
            dve.wait_ge(s_ident, 1)
            nc.vector.tensor_copy(ident_h[:, :], ident[:, :])
            nc.vector.tensor_tensor(fold[:, :], ident[0:SK, 0:FIELDS], ident[0:SK, FIELDS:2 * FIELDS],
                                    ALU.add).then_inc(s_const, 1)
            dve.wait_ge(s_const, 1)
            for c in range(2):
                nc.vector.tensor_tensor(unit[:, c * FIELDS:(c + 1) * FIELDS], fold[:, :],
                                        ident[0:SK, 2 * FIELDS:3 * FIELDS], ALU.add).then_inc(s_const, 1)
            dve.wait_ge(s_const, 3)
            nc.vector.tensor_copy(sel_rot[:, 0, :].rearrange("p (q m) -> p q m", q=RQ),
                                  unit[:, 0:FIELDS].unsqueeze(1).to_broadcast([SK, RQ, FIELDS]))
            for j in range(NROT):
                nc.vector.tensor_copy(sel_rot[:, 1 + j // RQ, (j % RQ) * FIELDS:(j % RQ + 1) * FIELDS],
                                      unit[:, j:j + FIELDS])
            nc.vector.tensor_copy(sel_row[:, :, :].rearrange("p t (c h) -> p (t c) h", h=HID),
                                  unit[:, 0:FIELDS].unsqueeze(2).to_broadcast([SK, FIELDS, HID])).then_inc(s_sel, 1)
            dve.wait_ge(s_w0, 2 * RQ * 16)
            for q in range(RQ):
                at = slice(q * FIELDS, (q + 1) * FIELDS)
                ts = [t for t in range(ROTS) if 1 <= t * RQ + q <= SYM]
                span = slice(ts[0], ts[-1] + 1)
                last = nc.vector.tensor_tensor(w0[at, span, :], w0[at, span, :], w0_mirror[at, span, :], ALU.add)
            last.then_inc(s_w0sum, 1)

            def pairs(p, k, n):
                dve.wait_ge(s_copied, job_no(p - 1, ROT_JOB + 1 + k) + 1)
                if k < RING:
                    wait_for(dve, s_used, n - RING + 1)
                nc.vector.tensor_tensor(prod[:, k, :], rots[:, 0, :], rots[:, 1 + k, :], ALU.mult).then_inc(s_prod, 1)

            def outer(p, t, x, n, back=RING):
                dve.wait_ge(s_copied, row_job(p, t) + 1)
                wait_for(dve, s_used, n - back + 1)
                nc.vector.tensor_tensor(prod[:, t % RING, :], rows[:, t, :], x[:, :], ALU.mult).then_inc(s_prod, 1)

            def period(p, last=False):
                dve.wait_ge(s_x1, p + 1)
                for t in range(ROWS):
                    outer(p, t, x1, step_no(p, A0 + t))
                if not last:
                    for k in range(ROTS):
                        pairs(p + 1, k, step_no(p, B0 + k))
                dve.wait_ge(s_x2, p + 1)
                for t in range(ROWS):
                    outer(p, t, x2, step_no(p, C0 + t, last), RING + (t < RING and not last))

            for k in range(ROTS):
                pairs(0, k, k)
            period(0)
            period(1)
            with dve.Fori(1, TILES - 1) as i:
                period(i * PAR)
                period(i * PAR + 1)
            period(TILES * PAR - 2)
            period(TILES * PAR - 1, last=True)

        @block.tensor
        def _(pe):
            def spread_job(kind, k, n, buf, par):
                wait_for(pe, s_copied, n if (kind, k) == ("rot", 0) else n - 1)
                out = spread[buf]
                if kind == "stack":
                    lhs = parts[:, :, :].rearrange("b s (m d) -> b s m d", d=EMB)
                    for d in range(ND):
                        last = nc.tensor.matmul(out[0:SK, d * BT:(d + 1) * BT], lhs[:, :, :, par * ND + d],
                                                ident_h[:, :], start=True, stop=True)
                else:
                    sel = sel_row if kind == "row" else sel_rot
                    for c in range(2):
                        cols = slice(c * HALF, (c + 1) * HALF)
                        last = nc.tensor.matmul(out[:, cols], sel[:, k, :], stack[:, cols], start=True, stop=True)
                last.then_inc(s_spread, 1)

            def contract(acc, w, buf, n, first, last):
                pe.wait_ge(s_prod, n + 1)
                for c in range(2):
                    mm = nc.tensor.matmul(acc[c * HID:(c + 1) * HID, :], w, prod[:, buf, c * HALF:(c + 1) * HALF],
                                          start=first, stop=last)
                mm.then_inc(s_used, 1)

            def layer0(k, n):
                contract(acc0, w0[:, k, :], k, n, k == 0, k == ROTS - 1)

            def tower_step(i, stage):
                if stage == 0:
                    pe.wait_ge(s_dense, (i + 1) * 16)
                    mm = nc.tensor.matmul(tower[0:CTX, 0:BT], dense[:, :], ident[:, :], start=True, stop=True)
                else:
                    pe.wait_ge(s_act, i * 4 + stage)
                if stage == 1:
                    pe.wait_ge(s_sum1, (i + 1) * PAR)
                    pe.wait_ge(s_sum2, (i + 1) * PAR)
                    pe.wait_ge(s_sum3, (i + 1) * PAR)
                    for m in range(TOP1 // P):
                        cols = slice(m * P, (m + 1) * P)
                        nc.tensor.matmul(tower[:, cols], t1a[:, cols], za[:, :], start=True, stop=False)
                        mm = nc.tensor.matmul(tower[:, cols], t1b[:, cols], zb[:, :], start=False, stop=True)
                if stage == 2:
                    for m in range(TOP2 // P):
                        cols = slice(m * P, (m + 1) * P)
                        for k in range(TOP1 // P):
                            mm = nc.tensor.matmul(tower[:, cols], t2[:, k, cols], h1[:, k, :],
                                                  start=(k == 0), stop=(k == TOP1 // P - 1))
                if stage == 3:
                    for k in range(TOP2 // P):
                        mm = nc.tensor.matmul(tower[0:1, 0:BT], t3[:, k:k + 1], h2[:, k, :],
                                              start=(k == 0), stop=(k == TOP2 // P - 1))
                mm.then_inc(s_tower, 1)

            def period(i, par, first=False, last=False):
                p = i * PAR + par
                j = 0
                for s in range(STEPS):
                    n = step_no(p, s, last)
                    if s < B0:
                        if s == A0:
                            wait_for(pe, s_x2, p)
                        contract(acc1, w1[:, s, :], s % RING, n, s == 0, s == ROWS - 1)
                    elif s < C0:
                        if not last:
                            if s == B0:
                                pe.wait_ge(s_x1, p + 1)
                            layer0(s - B0, n)
                    else:
                        if s == C0:
                            wait_for(pe, s_x3, p)
                        contract(acc2, w2[:, s - C0, :], (s - C0) % RING, n, s == C0, s == STEPS - 1)
                    for kind, k in JOBS[s]:
                        now = s < ROWS - EARLY
                        if last and not now:
                            continue
                        if kind == "stack" and par == 1:
                            pe.wait_ge(s_parts, i + 2)
                        spread_job(kind, k, job_no(p, j), (PER_PERIOD * par + j) % 2, par if now else 1 - par)
                        j += 1
                    if par == 0 and not first and s in TOWER_AT:
                        tower_step(i - 1, TOWER_AT[s])

            pe.wait_ge(s_sel, 1)
            pe.wait_ge(s_parts, 1)
            for n in range(3):
                spread_job(*FIRST_JOBS[n], n, n % 2, 0)
            pe.wait_ge(s_w0sum, 1)
            for k in range(ROTS):
                if k + 1 < ROTS:
                    spread_job(*FIRST_JOBS[3 + k], 3 + k, (3 + k) % 2, 0)
                layer0(k, k)
            for n in range(2 + ROTS, len(FIRST_JOBS)):
                spread_job(*FIRST_JOBS[n], n, n % 2, 0)
            pe.wait_ge(s_w12, 32)
            pe.wait_ge(s_top, 6 * 16)
            period(0, 0, first=True)
            period(0, 1)
            with pe.Fori(1, TILES - 1) as i:
                period(i, 0)
                period(i, 1)
            period(TILES - 1, 0)
            period(TILES - 1, 1, last=True)
            for stage in range(4):
                tower_step(TILES - 1, stage)

        @block.scalar
        def _(act):
            def copy_job(kind, k, n, buf, p):
                act.wait_ge(s_spread, n + 1)
                if kind == "stack":
                    nc.scalar.activation(stack[:, :], spread[buf][0:SK, :], ACT.Copy).then_inc(s_copied, 1)
                elif kind == "rot":
                    if not (isinstance(p, int) and p == 0):
                        wait_for(act, s_prod, ROTS if isinstance(p, int) and p == 1 else step_no(p - 2, B0 + ROTS - 1) + 1)
                    nc.scalar.activation(rots[:, k, :], spread[buf][:, :], ACT.Copy).then_inc(s_copied, 1)
                else:
                    if not (isinstance(p, int) and p == 0):
                        act.wait_ge(s_prod, step_no(p - 1, C0 + k) + 1)
                    nc.scalar.activation(rows[:, k, :], spread[buf][:, :], ACT.Copy).then_inc(s_copied, 1)

            def relu_twice(x, acc, done):
                for c in range(2):
                    for h in range(2):
                        last = nc.scalar.activation(x[h * HID:(h + 1) * HID, c * HALF:(c + 1) * HALF],
                                                    acc[c * HID:(c + 1) * HID, :], ACT.Relu)
                last.then_inc(done, 1)

            def relu1(p, n):
                act.wait_ge(s_used, n + 1)
                if not (isinstance(p, int) and p == 0):
                    act.wait_ge(s_prod, step_no(p - 1, A0 + ROWS - 1) + 1)
                    act.wait_ge(s_sum1, p)
                relu_twice(x1, acc0, s_x1)

            def relu2(p):
                act.wait_ge(s_used, step_no(p, A0 + ROWS - 1) + 1)
                if not (isinstance(p, int) and p == 0):
                    act.wait_ge(s_prod, step_no(p - 1, STEPS - 1) + 1)
                    act.wait_ge(s_sum2, p)
                relu_twice(x2, acc1, s_x2)

            def relu3(p, last=False):
                act.wait_ge(s_used, step_no(p, STEPS - 1, last) + 1)
                if not (isinstance(p, int) and p == 0):
                    act.wait_ge(s_sum3, p)
                for c in range(2):
                    done = nc.scalar.activation(x3[:, c * HALF:(c + 1) * HALF], acc2[c * HID:(c + 1) * HID, :], ACT.Relu)
                done.then_inc(s_x3, 1)

            def tower_step(i, stage):
                act.wait_ge(s_tower, i * 4 + stage + 1)
                if stage == 0:
                    done = nc.scalar.activation(zb[HID:HID + CTX, :], tower[0:CTX, 0:BT], ACT.Copy)
                if stage == 1:
                    for m in range(TOP1 // P):
                        done = nc.scalar.activation(h1[:, m, :], tower[:, m * P:(m + 1) * P], ACT.Relu, bias=b1[:, m:m + 1])
                if stage == 2:
                    for m in range(TOP2 // P):
                        done = nc.scalar.activation(h2[:, m, :], tower[:, m * P:(m + 1) * P], ACT.Relu, bias=b2[:, m:m + 1])
                if stage == 3:
                    done = nc.scalar.activation(yv[:, :], tower[0:1, 0:BT], ACT.Copy)
                done.then_inc(s_act, 1)

            def period(i, par, first=False, last=False):
                p = i * PAR + par
                j = 0
                for s in range(STEPS):
                    if s == 0 and not first:
                        relu3(p - 1)
                    if s == B0 - 1:
                        relu2(p)
                    if s == C0 - 1 and not last:
                        relu1(p + 1, step_no(p, s))
                    for kind, k in JOBS[s]:
                        now = s < ROWS - EARLY
                        if last and not now:
                            continue
                        copy_job(kind, k, job_no(p, j), (PER_PERIOD * par + j) % 2, p if now else p + 1)
                        j += 1
                    if par == 0 and not first and s in TOWER_AT:
                        tower_step(i - 1, TOWER_AT[s])

            for n in range(2 + ROTS):
                copy_job(*FIRST_JOBS[n], n, n % 2, 0)
            relu1(0, ROTS - 1)
            for n in range(2 + ROTS, len(FIRST_JOBS)):
                copy_job(*FIRST_JOBS[n], n, n % 2, 0)
            act.wait_ge(s_top, 6 * 16)
            period(0, 0, first=True)
            period(0, 1)
            with act.Fori(1, TILES - 1) as i:
                period(i, 0)
                period(i, 1)
            period(TILES - 1, 0)
            period(TILES - 1, 1, last=True)
            relu3(TILES * PAR - 1, last=True)
            for stage in range(4):
                tower_step(TILES - 1, stage)


def kernel(**inputs):
    import numpy as np
    import concourse.bacc as bacc
    from concourse.bass_utils import run_bass_kernel_spmd

    nc = bacc.Bacc("TRN2", target_bir_lowering=False, num_devices=1)
    arrays, aps = {}, {}
    for name, value in inputs.items():
        a = np.ascontiguousarray(value)
        arrays[f"in_{name}"] = a
        aps[name] = nc.dram_tensor(f"in_{name}", a.shape, mybir.dt.from_np(a.dtype), kind="ExternalInput").ap()
    batch, fields = inputs["ids"].shape
    y = nc.dram_tensor("out_y", (batch, 1), mybir.dt.float32, kind="ExternalOutput").ap()
    cin_tower_kernel(nc, aps["dense_ctx"], aps["ids"], [aps[f"tbl_{f}"] for f in range(fields)],
                     aps["W_top1"], aps["b_top1"], aps["W_top2"], aps["b_top2"], aps["W_top3"],
                     aps["L0_rec_W0"], aps["L0_rec_W1"], aps["L0_rec_W2"], y)
    return run_bass_kernel_spmd(nc, [arrays], core_ids=[0]).results[0]["out_y"]
```

```python
import concourse.bass as bass
from concourse import mybir
from contextlib import ExitStack


def cin_tower_kernel(nc, dense_ctx, ids, tables, w_top1, b_top1, w_top2, b_top2, w_top3,
                     w_cin0, w_cin1, w_cin2, y_out):
    fp32, bf16, i32 = mybir.dt.float32, mybir.dt.bfloat16, mybir.dt.int32
    ALU, ACT = mybir.AluOpType, mybir.ActivationFunctionType

    P = 128
    BATCH, FIELDS = ids.shape
    EMB = tables[0].shape[1]
    HID = w_cin1.shape[2]
    CTX = dense_ctx.shape[1]
    TOP1, TOP2 = w_top1.shape[1], w_top2.shape[1]

    BT = P
    TILES = BATCH // BT
    PAR = 2
    HALF = 512
    N = 2 * HALF
    DQ = HALF // BT
    ND = N // BT
    PARTS = 3
    SK = PARTS * FIELDS

    ROWS = FIELDS * HID // P
    ROTS = 5
    RQ = P // FIELDS
    NROT = ROTS * RQ
    SYM = FIELDS - NROT

    DMA_ROWS = 12
    GROUP = 4
    GROUPS = DMA_ROWS // GROUP

    AHEAD = 4
    N0, C0 = ROWS - AHEAD, ROWS
    STEPS = 2 * ROWS
    RING = 4

    JOBS = [[] for _ in range(STEPS)]
    for t in range(DMA_ROWS, ROWS):
        at = C0 + t + 2
        JOBS[at % STEPS].append(("row", t, 1 if at < STEPS else 0))
    JOBS[C0 + 1].append(("stack", 0, 2))
    JOBS[C0 + 3].append(("field", 0, 2))
    for k in range(ROTS):
        JOBS[C0 + 4 + 2 * k].append(("rot", k, 2))
    SUM0_AT = {s: s for s in range(ROTS)}
    PROLOGUE = [("stack", 0, 0), ("field", 0, 0)] + [("rot", k, 0) for k in range(ROTS)]
    LATER = [("row", t, 0) for t in range(DMA_ROWS, ROWS) if C0 + t + 2 < STEPS]
    FIRST_JOBS = [list(x) for x in JOBS]
    FIRST_JOBS[1].append(("stack", 0, 1))
    FIRST_JOBS[2].append(("field", 0, 1))
    for k in range(ROTS):
        FIRST_JOBS[3 + k].append(("rot", k, 1))
    FIRST_SUM0_AT = {5 + k: k for k in range(ROTS)}

    TOWER_AT = {14: 0, 17: 1, 20: 2, 23: 3}
    PERIODS = TILES * PAR

    def jobs_of(p, s):
        found = FIRST_JOBS[s] if p == 0 else JOBS[s]
        return [(kind, k, up) for kind, k, up in found if p is None or p + up < PERIODS]

    NUMBER = {}
    for kind, k, p in PROLOGUE + LATER:
        NUMBER[kind, k, p] = len(NUMBER)
    for p in range(PERIODS):
        for s in range(STEPS):
            for kind, k, up in jobs_of(p, s):
                NUMBER[kind, k, p + up] = len(NUMBER)
    PER_PERIOD = sum(len(x) for x in JOBS)

    def job_no(kind, k, p):
        return NUMBER[kind, k, p] if isinstance(p, int) else NUMBER[kind, k, 4] + (p - 4) * PER_PERIOD

    def job_buffer(kind, k, par, p):
        return job_no(kind, k, p if isinstance(p, int) else 4 + par) % 2

    def step_no(p, s, last=False):
        return p * STEPS + AHEAD + s - (AHEAD if last and s >= C0 else 0)

    def slot(par, t):
        return par * DMA_ROWS + t if t < DMA_ROWS else DMA_ROWS + t

    def wait_for(eng, sem, value):
        if isinstance(value, int) and value <= 0:
            return
        eng.wait_ge(sem, value)

    with ExitStack() as ctx:
        def sb(name, shape, dt=fp32):
            return ctx.enter_context(nc.sbuf_tensor(name, shape, dt))

        def sem(name):
            return ctx.enter_context(nc.semaphore(name))

        w0 = sb("w0", [P, ROTS, HID])
        w1 = sb("w1", [P, ROWS, HID])
        w2 = sb("w2", [P, ROWS, HID])
        t1a = sb("t1a", [P, TOP1])
        t1b = sb("t1b", [HID + CTX, TOP1])
        t2 = sb("t2", [P, TOP1 // P, TOP2])
        t3 = sb("t3", [P, TOP2 // P])
        b1 = sb("b1", [P, TOP1 // P])
        b2 = sb("b2", [P, TOP2 // P])
        ident = sb("ident", [P, P])
        ident_h = sb("ident_h", [P, P], bf16)
        fold = sb("fold", [SK, FIELDS])
        unit = sb("unit", [SK, 2 * FIELDS], bf16)
        sel_row = sb("sel_row", [SK, ROWS - DMA_ROWS, P], bf16)
        sel_rot = sb("sel_rot", [SK, ROTS, P], bf16)
        row_col = sb("row_col", [FIELDS, 2, HID])
        idx = sb("idx", [P, FIELDS], i32)
        emb = sb("emb", [P, FIELDS * EMB])
        zero = sb("zero", [P, 1])
        parts = sb("parts", [P, PARTS, FIELDS * EMB], bf16)
        dense = sb("dense", [P, CTX])
        stack = [sb(f"stack{n}", [SK, N], bf16) for n in range(2)]
        x3_field = sb("x3_field", [HID + FIELDS, N])
        x3, field = x3_field[0:HID, :], x3_field[HID:HID + FIELDS, :]
        rows = sb("rows", [P, DMA_ROWS + ROWS, N])
        squares = sb("squares", [P, ROTS, N])
        prod = sb("prod", [P, RING, N])
        x1 = [sb(f"x1{n}", [P, N]) for n in "ab"]
        x2 = sb("x2", [P, N])
        tmp = sb("tmp", [P, HALF + HALF // 2])
        rest = tmp[:, 0:FIELDS * EMB]
        half_sum = sb("half_sum", [P, 3, BT])
        za = sb("za", [P, BT])
        zb = sb("zb", [HID + CTX, BT])
        h1 = sb("h1", [P, TOP1 // P, BT])
        w0_mirror = h1[:, :, :].rearrange("p m b -> p (m b)")[:, 0:ROTS * HID].rearrange("p (t k) -> p t k", k=HID)
        h2 = sb("h2", [P, TOP2 // P, BT])
        yv = sb("yv", [1, BT])

        spread = [ctx.enter_context(nc.psum_tensor(f"spread{i}", [P, N], fp32)) for i in range(2)]
        acc0 = ctx.enter_context(nc.psum_tensor("acc0", [P, HALF], fp32))
        acc1 = [ctx.enter_context(nc.psum_tensor(f"acc1{n}", [P, HALF], fp32)) for n in "ab"]
        acc2 = ctx.enter_context(nc.psum_tensor("acc2", [P, HALF], fp32))
        tower = acc0

        w0_wide = nc.dram_tensor("w0_wide", [FIELDS, 2 * FIELDS, HID], fp32, kind="Internal").ap()
        w0_tall = nc.dram_tensor("w0_tall", [2 * FIELDS, FIELDS, HID], fp32, kind="Internal").ap()

        field_dram = nc.dram_tensor("field_dram", [2, FIELDS, N], fp32, kind="Internal").ap()

        s_wide = sem("s_wide")
        s_w0 = sem("s_w0")
        s_w12 = sem("s_w12")
        s_top = sem("s_top")
        s_idx = sem("s_idx")
        s_dense = sem("s_dense")
        s_ident0 = sem("s_ident0")
        s_ident = sem("s_ident")
        s_const = sem("s_const")
        s_sel = sem("s_sel")
        s_w0sum = sem("s_w0sum")
        s_gather = sem("s_gather")
        s_split = sem("s_split")
        s_add = [sem(f"s_add{n}") for n in range(1, 4)]
        s_parts = sem("s_parts")
        s_spread = sem("s_spread")
        s_copied = sem("s_copied")
        s_prod = sem("s_prod")
        s_field = sem("s_field")
        s_rows = [sem(f"s_rows{g}") for g in range(GROUPS)]
        s_sum0 = sem("s_sum0")
        s_w0loads = sem("s_w0loads")
        s_used = sem("s_used")
        s_x1 = sem("s_x1")
        s_x2 = sem("s_x2")
        s_x3 = sem("s_x3")
        s_sum1 = sem("s_sum1")
        s_sum2 = sem("s_sum2")
        s_sum3 = sem("s_sum3")
        s_tower = sem("s_tower")
        s_act = sem("s_act")
        s_y = sem("s_y")

        block = ctx.enter_context(nc.Block())

        @block.sync
        def _(sp):
            def load_tile(i):
                if not (isinstance(i, int) and i == 0):
                    sp.wait_ge(s_gather, i * FIELDS * 16)
                sp.dma_start(idx[:, :], ids[bass.ts(i, BT), :]).then_inc(s_idx, 16)

            def load_dense(i):
                sp.dma_start(dense[:, :], dense_ctx[bass.ts(i, BT), :]).then_inc(s_dense, 16)

            def store(i):
                sp.wait_ge(s_act, (i + 1) * 4)
                sp.dma_start(y_out[bass.ts(i, BT), :].rearrange("b o -> o b"), yv[:, :]).then_inc(s_y, 16)
                sp.wait_ge(s_y, (i + 1) * 16)

            def field_out(p, par):
                sp.wait_ge(s_copied, job_no("field", 0, p) + 1)
                sp.dma_start(field_dram[par, :, :], field[:, :]).then_inc(s_field, 16)
                sp.wait_ge(s_field, (p + 1) * 16)

            def rows_in(p, par):
                for g in range(GROUPS):
                    if g > 0 and not (isinstance(p, int) and p < 2):
                        sp.wait_ge(s_prod, step_no(p - 2, C0 + g * GROUP + GROUP - 1) + 1)
                    first = slot(par, g * GROUP)
                    for c in range(2):
                        src = bass.AP(field_dram.tensor, (par * FIELDS + 2 * g * GROUP + c) * N,
                                      [[0, HID], [2 * N, GROUP], [1, N]])
                        sp.dma_start(rows[c * HID:(c + 1) * HID, first:first + GROUP, :], src).then_inc(s_rows[g], 16)

            load_tile(0)
            sp.dma_start(prod[0:FIELDS, 0:2, :].rearrange("a x y -> a (x y)"),
                         w_cin0.rearrange("a b k -> a (b k)")).then_inc(s_w0loads, 16)
            sp.dma_start(prod[0:FIELDS, 2:4, :].rearrange("b x y -> b (x y)").rearrange("b (a k) -> b a k", k=HID),
                         w_cin0.rearrange("a b k -> b a k")).then_inc(s_w0loads, 16)
            for c in range(2):
                sp.dma_start(w0_wide[:, c * FIELDS:(c + 1) * FIELDS, :], w_cin0).then_inc(s_wide, 16)
                sp.dma_start(w0_tall[c * FIELDS:(c + 1) * FIELDS, :, :], w_cin0).then_inc(s_wide, 16)
            load_dense(0)
            sp.dma_start(w1[:, :, :], w_cin1.rearrange("m h k -> (m h) k").rearrange("(t p) k -> p t k", p=P)).then_inc(s_w12, 16)
            sp.dma_start(w2[:, :, :], w_cin2.rearrange("m h k -> (m h) k").rearrange("(t p) k -> p t k", p=P)).then_inc(s_w12, 16)
            sp.wait_ge(s_wide, 64)
            for q in range(RQ):
                at = slice(q * FIELDS, (q + 1) * FIELDS)
                sp.dma_start(w0[at, :, :], bass.AP(w0_wide.tensor, q * HID, [
                    [(2 * FIELDS + 1) * HID, FIELDS], [RQ * HID, ROTS], [1, HID]])).then_inc(s_w0, 16)
                sp.dma_start(w0_mirror[at, :, :], bass.AP(w0_tall.tensor, q * FIELDS * HID, [
                    [(FIELDS + 1) * HID, FIELDS], [RQ * FIELDS * HID, ROTS], [1, HID]])).then_inc(s_w0, 16)
            sp.dma_start(t1a[:, :], w_top1[0:P, :]).then_inc(s_top, 16)
            sp.dma_start(t1b[:, :], w_top1[P:, :]).then_inc(s_top, 16)
            sp.dma_start(t2[:, :, :], w_top2.rearrange("(t p) n -> p t n", p=P)).then_inc(s_top, 16)
            sp.dma_start(t3[:, :], w_top3.rearrange("(t p) o -> p (t o)", p=P),
                         allow_slow_non_contiguous=True).then_inc(s_top, 16)
            sp.dma_start(b1[:, :], b_top1.rearrange("(t p) -> p t", p=P),
                         allow_slow_non_contiguous=True).then_inc(s_top, 16)
            sp.dma_start(b2[:, :], b_top2.rearrange("(t p) -> p t", p=P),
                         allow_slow_non_contiguous=True).then_inc(s_top, 16)
            load_tile(1)
            for p in range(2):
                field_out(p, p)
                rows_in(p, p)

            def turn(i, ids_too=True, first=False, last=False):
                if ids_too and not first:
                    load_tile(i + 2)
                if not last:
                    field_out(i * PAR + 2, 0)
                    rows_in(i * PAR + 2, 0)
                if first:
                    load_tile(2)
                else:
                    store(i - 1)
                    load_dense(i)
                if not last:
                    field_out(i * PAR + 3, 1)
                    rows_in(i * PAR + 3, 1)

            turn(0, first=True)
            with sp.Fori(1, TILES - 2) as i:
                turn(i)
            turn(TILES - 2, ids_too=False)
            turn(TILES - 1, ids_too=False, last=True)
            store(TILES - 1)

        @block.gpsimd
        def _(pool):
            nc.gpsimd.memset(zero[:, :], 0.0).then_inc(s_ident0, 1)
            zeros = zero[:, :].to_broadcast([P, FIELDS * EMB])
            nc.gpsimd.memset(ident[:, :], 0.0).then_inc(s_ident0, 1)
            pool.wait_ge(s_ident0, 2)
            nc.gpsimd.affine_select(out=ident[:, :], in_=ident[:, :], compare_op=ALU.not_equal, fill=1.0,
                                    base=0, pattern=[[-1, P]], channel_multiplier=1).then_inc(s_ident, 1)

            def gather(i):
                pool.drain()
                for f in range(FIELDS):
                    pool.indirect_dma_start(
                        out=emb[:, f * EMB:(f + 1) * EMB], out_offset=None, in_=tables[f],
                        in_offset=bass.IndirectOffsetOnAxis(ap=idx[:, f:f + 1], axis=0)).then_inc(s_gather, 16)

            def split(i):
                pool.drain()
                if not (isinstance(i, int) and i == 0):
                    pool.wait_ge(s_spread, job_no("stack", 0, (i - 1) * PAR + 1) + 1)
                nc.gpsimd.tensor_tensor(parts[:, 0, :], emb[:, :], zeros, ALU.add).then_inc(s_split, 1)
                pool.wait_ge(s_split, i * 3 + 1)
                nc.gpsimd.tensor_tensor(rest[:, :], emb[:, :], parts[:, 0, :], ALU.subtract).then_inc(s_split, 1)
                pool.wait_ge(s_split, i * 3 + 2)
                nc.gpsimd.tensor_tensor(parts[:, 1, :], rest[:, :], zeros, ALU.add).then_inc(s_split, 1)
                pool.wait_ge(s_split, i * 3 + 3)
                nc.gpsimd.tensor_tensor(parts[:, 2, :], rest[:, :], parts[:, 1, :], ALU.subtract).then_inc(s_parts, 1)

            def sum_d(x, lo, layer, i, par, out, done):
                r = slice(lo, lo + HID)
                q = HALF // 2
                add, base = s_add[layer], i * 5 + 2 * par
                t = tmp
                nc.gpsimd.tensor_tensor(t[r, 0:HALF], x[r, 0:HALF], x[r, HALF:N], ALU.add).then_inc(add, 1)
                pool.wait_ge(add, base + 1)
                nc.gpsimd.tensor_tensor(t[r, HALF:HALF + q], t[r, 0:q], t[r, q:HALF], ALU.add).then_inc(add, 1)
                pool.wait_ge(add, base + 2)
                a, b = t[r, HALF:HALF + BT], t[r, HALF + BT:HALF + q]
                if par == 0:
                    nc.gpsimd.tensor_tensor(half_sum[r, layer, :], a, b, ALU.add).then_inc(done, 1)
                else:
                    nc.gpsimd.tensor_tensor(t[r, 0:BT], a, b, ALU.add).then_inc(add, 1)
                    pool.wait_ge(add, base + 3)
                    nc.gpsimd.tensor_tensor(out, t[r, 0:BT], half_sum[r, layer, :], ALU.add).then_inc(done, 1)

            def sum1(i, par, *also):
                pool.drain()
                for sem_, value in also:
                    pool.wait_ge(sem_, value)
                pool.wait_ge(s_x1, i * PAR + par + 1)
                sum_d(x1[par], 0, 0, i, par, za[0:HID, :], s_sum1)

            def sum2(i, par, *also):
                pool.drain()
                for sem_, value in also:
                    pool.wait_ge(sem_, value)
                pool.wait_ge(s_x2, i * PAR + par + 1)
                sum_d(x2, HID, 1, i, par, za[HID:P, :], s_sum2)

            def sum3(i, par, *also):
                pool.drain()
                for sem_, value in also:
                    pool.wait_ge(sem_, value)
                pool.wait_ge(s_x3, i * PAR + par + 1)
                sum_d(x3, 0, 2, i, par, zb[0:HID, :], s_sum3)

            def turn(i, more=True, first=False):
                if not first:
                    sum3(i - 1, 1)
                sum1(i, 0)
                sum2(i, 0)
                sum3(i, 0)
                if more:
                    sum1(i, 1, (s_idx, (i + 3) * 16))
                    gather(i + 2)
                    sum2(i, 1, (s_gather, (i + 3) * FIELDS * 16))
                    split(i + 2)
                else:
                    sum1(i, 1)
                    sum2(i, 1)

            for i in range(2):
                pool.wait_ge(s_idx, (i + 1) * 16)
                gather(i)
                pool.wait_ge(s_gather, (i + 1) * FIELDS * 16)
                split(i)
            turn(0, first=True)
            with pool.Fori(1, TILES - 2) as i:
                turn(i)
            turn(TILES - 2, more=False)
            turn(TILES - 1, more=False)
            sum3(TILES - 1, 1)

        @block.vector
        def _(dve):
            dve.wait_ge(s_ident, 1)
            nc.vector.tensor_copy(ident_h[:, :], ident[:, :])
            nc.vector.tensor_tensor(fold[:, :], ident[0:SK, 0:FIELDS], ident[0:SK, FIELDS:2 * FIELDS],
                                    ALU.add).then_inc(s_const, 1)
            dve.wait_ge(s_const, 1)
            for c in range(2):
                nc.vector.tensor_tensor(unit[:, c * FIELDS:(c + 1) * FIELDS], fold[:, :],
                                        ident[0:SK, 2 * FIELDS:3 * FIELDS], ALU.add).then_inc(s_const, 1)
            dve.wait_ge(s_const, 3)
            for j in range(NROT):
                nc.vector.tensor_tensor(sel_rot[:, j // RQ, (j % RQ) * FIELDS:(j % RQ + 1) * FIELDS],
                                        unit[:, 0:FIELDS], unit[:, j:j + FIELDS], ALU.add)
            nc.vector.tensor_copy(sel_row[:, :, :].rearrange("p t (c h) -> p (t c) h", h=HID),
                                  unit[:, 2 * DMA_ROWS:FIELDS].unsqueeze(2)
                                  .to_broadcast([SK, FIELDS - 2 * DMA_ROWS, HID])).then_inc(s_sel, 1)
            dve.wait_ge(s_w0, 2 * RQ * 16)
            for q in range(RQ):
                at = slice(q * FIELDS, (q + 1) * FIELDS)
                ts = [t for t in range(ROTS) if 1 <= t * RQ + q <= SYM]
                span = slice(ts[0], ts[-1] + 1)
                last = nc.vector.tensor_tensor(w0[at, span, :], w0[at, span, :], w0_mirror[at, span, :], ALU.add)
            last.then_inc(s_const, 1)
            dve.wait_ge(s_w0loads, 32)
            for c in range(2):
                nc.vector.tensor_reduce(row_col[:, c, :], prod[0:FIELDS, 2 * c:2 * c + 2, :]
                                        .rearrange("a x y -> a (x y)").rearrange("a (b k) -> a k b", k=HID),
                                        mybir.AxisListType.X, ALU.add).then_inc(s_const, 1)
            dve.wait_ge(s_const, 6)
            nc.vector.tensor_scalar(w0[:, :, :], w0[:, :, :], 0.5, None, ALU.mult).then_inc(s_const, 1)
            nc.vector.tensor_tensor(row_col[:, 0, :], row_col[:, 0, :], row_col[:, 1, :], ALU.add).then_inc(s_const, 1)
            dve.wait_ge(s_const, 8)
            nc.vector.scalar_tensor_tensor(out=w0[0:FIELDS, 0, :], in0=row_col[:, 0, :], scalar=-0.125,
                                           in1=w0[0:FIELDS, 0, :], op0=ALU.mult, op1=ALU.add).then_inc(s_w0sum, 1)

            def outer(p, par, layer, t, n):
                if layer == 1 and t >= DMA_ROWS:
                    dve.wait_ge(s_copied, job_no("row", t, p) + 1)
                if layer == 1 and t < DMA_ROWS and t % GROUP == 0:
                    dve.wait_ge(s_rows[t // GROUP], (p + 1) * 32)
                if layer == 1 and t == 0:
                    dve.wait_ge(s_x1, p + 1)
                if layer == 2 and t == 0:
                    dve.wait_ge(s_x2, p + 1)
                wait_for(dve, s_used, n - RING + 1)
                nc.vector.tensor_tensor(prod[:, t % RING, :], rows[:, slot(par, t), :],
                                        x1[par][:, :] if layer == 1 else x2[:, :], ALU.mult).then_inc(s_prod, 1)

            def period(i, par, last=False):
                p = i * PAR + par
                for t in range(AHEAD, ROWS):
                    outer(p, par, 1, t, step_no(p, t - AHEAD))
                if not last:
                    for t in range(AHEAD):
                        outer(p + 1, 1 - par, 1, t, step_no(p, N0 + t))
                for t in range(ROWS):
                    outer(p, par, 2, t, step_no(p, C0 + t, last))

            for t in range(AHEAD):
                outer(0, 0, 1, t, t)
            period(0, 0)
            period(0, 1)
            with dve.Fori(1, TILES - 1) as i:
                period(i, 0)
                period(i, 1)
            period(TILES - 1, 0)
            period(TILES - 1, 1, last=True)

        @block.tensor
        def _(pe):
            def job(kind, k, p, par):
                n = job_no(kind, k, p)
                wait_for(pe, s_copied, job_no("stack", 0, p) + 1 if kind == "field" else n - 1)
                out = spread[job_buffer(kind, k, par, p)]
                if kind == "stack":
                    lhs = parts[:, :, :].rearrange("b s (m d) -> b s m d", d=EMB)
                    for d in range(ND):
                        last = nc.tensor.matmul(out[0:SK, d * BT:(d + 1) * BT], lhs[:, :, :, par * ND + d],
                                                ident_h[:, :], start=True, stop=True)
                else:
                    if kind == "row":
                        sel = sel_row[:, k - DMA_ROWS, :]
                    else:
                        sel = unit[:, 0:FIELDS] if kind == "field" else sel_rot[:, k, :]
                    m = FIELDS if kind == "field" else P
                    for c in range(2):
                        cols = slice(c * HALF, (c + 1) * HALF)
                        last = nc.tensor.matmul(out[0:m, cols], sel, stack[par][:, cols], start=True, stop=True)
                last.then_inc(s_spread, 1)

            def contract(acc, w, operand, first, last):
                for c in range(2):
                    mm = nc.tensor.matmul(acc[c * HID:(c + 1) * HID, :], w, operand[:, c * HALF:(c + 1) * HALF],
                                          start=first, stop=last)
                return mm

            def layer0(k, p):
                pe.wait_ge(s_copied, job_no("rot", k, p) + 1)
                mm = contract(acc0, w0[:, k, :], squares[:, k, :], k == 0, k == ROTS - 1)
                if k == ROTS - 1:
                    mm.then_inc(s_sum0, 1)

            def outer(w, t, acc, n):
                pe.wait_ge(s_prod, n + 1)
                contract(acc, w[:, t, :], prod[:, t % RING, :], t == 0, t == ROWS - 1).then_inc(s_used, 1)

            def tower_step(i, stage):
                if stage == 0:
                    pe.wait_ge(s_dense, (i + 1) * 16)
                    wait_for(pe, s_x1, min((i + 1) * PAR + 2, PERIODS) if isinstance(i, int) else (i + 1) * PAR + 2)
                    mm = nc.tensor.matmul(tower[0:CTX, 0:BT], dense[:, :], ident[:, :], start=True, stop=True)
                else:
                    pe.wait_ge(s_act, i * 4 + stage)
                if stage == 1:
                    pe.wait_ge(s_sum1, (i + 1) * PAR)
                    pe.wait_ge(s_sum2, (i + 1) * PAR)
                    pe.wait_ge(s_sum3, (i + 1) * PAR)
                    for m in range(TOP1 // P):
                        cols = slice(m * P, (m + 1) * P)
                        nc.tensor.matmul(tower[:, cols], t1a[:, cols], za[:, :], start=True, stop=False)
                        mm = nc.tensor.matmul(tower[:, cols], t1b[:, cols], zb[:, :], start=False, stop=True)
                if stage == 2:
                    for m in range(TOP2 // P):
                        cols = slice(m * P, (m + 1) * P)
                        for k in range(TOP1 // P):
                            mm = nc.tensor.matmul(tower[:, cols], t2[:, k, cols], h1[:, k, :],
                                                  start=(k == 0), stop=(k == TOP1 // P - 1))
                if stage == 3:
                    for k in range(TOP2 // P):
                        mm = nc.tensor.matmul(tower[0:1, 0:BT], t3[:, k:k + 1], h2[:, k, :],
                                              start=(k == 0), stop=(k == TOP2 // P - 1))
                mm.then_inc(s_tower, 1)

            def period(i, par, first=False, last=False):
                p = i * PAR + par
                for s in range(STEPS):
                    if s < N0:
                        outer(w1, s + AHEAD, acc1[par], step_no(p, s))
                    elif s < C0:
                        if s == N0:
                            wait_for(pe, s_x2, p)
                        if not last:
                            outer(w1, s - N0, acc1[1 - par], step_no(p, s))
                    else:
                        if s == C0:
                            wait_for(pe, s_x3, p)
                        outer(w2, s - C0, acc2, step_no(p, s, last))
                    for kind, k, up in jobs_of(p if isinstance(p, int) else None, s):
                        if kind == "stack" and par == 0 and up == PAR:
                            pe.wait_ge(s_parts, i + 2)
                        job(kind, k, p + up, (par + up) % 2)
                    k = (FIRST_SUM0_AT if first else SUM0_AT).get(s)
                    if k is not None and not last:
                        if k == 0:
                            pe.wait_ge(s_x1, p + 1)
                            if par == 1 and not first and not (isinstance(i, int) and i == 0):
                                pe.wait_ge(s_act, i * 4)
                        layer0(k, p + 1)
                    if par == 0 and not first and s in TOWER_AT:
                        tower_step(i - 1, TOWER_AT[s])

            pe.wait_ge(s_sel, 1)
            pe.wait_ge(s_parts, 1)
            for kind, k, p in PROLOGUE:
                job(kind, k, p, p)
            pe.wait_ge(s_w0sum, 1)
            for k in range(ROTS):
                layer0(k, 0)
            for kind, k, p in LATER:
                job(kind, k, p, p)
            pe.wait_ge(s_w12, 32)
            pe.wait_ge(s_top, 6 * 16)
            for t in range(AHEAD):
                outer(w1, t, acc1[0], t)
            period(0, 0, first=True)
            period(0, 1)
            with pe.Fori(1, TILES - 1) as i:
                period(i, 0)
                period(i, 1)
            period(TILES - 1, 0)
            period(TILES - 1, 1, last=True)
            for stage in range(4):
                tower_step(TILES - 1, stage)

        @block.scalar
        def _(act):
            def job(kind, k, p, par):
                n = job_no(kind, k, p)
                got = spread[job_buffer(kind, k, par, p)]
                act.wait_ge(s_spread, n + 1)
                if kind == "stack":
                    done = nc.scalar.activation(stack[par][:, :], got[0:SK, :], ACT.Copy)
                elif kind == "field":
                    if not (isinstance(p, int) and p == 0):
                        act.wait_ge(s_field, p * 16)
                    done = nc.scalar.activation(field[:, :], got[0:FIELDS, :], ACT.Copy)
                elif kind == "rot":
                    wait_for(act, s_sum0, p)
                    done = nc.scalar.activation(squares[:, k, :], got[:, :], ACT.Square)
                else:
                    if not (isinstance(p, int) and p == 0):
                        act.wait_ge(s_prod, step_no(p - 1, C0 + k) + 1)
                    done = nc.scalar.activation(rows[:, slot(par, k), :], got[:, :], ACT.Copy)
                done.then_inc(s_copied, 1)

            def relu_twice(x, acc, done):
                for c in range(2):
                    for h in range(2):
                        last = nc.scalar.activation(x[h * HID:(h + 1) * HID, c * HALF:(c + 1) * HALF],
                                                    acc[c * HID:(c + 1) * HID, :], ACT.Relu)
                last.then_inc(done, 1)

            def relu1(p, par):
                act.wait_ge(s_sum0, p + 1)
                if not (isinstance(p, int) and p < 2):
                    act.wait_ge(s_prod, step_no(p - 2, N0 - 1) + 1)
                    act.wait_ge(s_sum1, p - 1)
                relu_twice(x1[par], acc0, s_x1)

            def relu2(p, par):
                act.wait_ge(s_used, step_no(p, N0 - 1) + 1)
                if not (isinstance(p, int) and p == 0):
                    act.wait_ge(s_prod, step_no(p - 1, STEPS - 1) + 1)
                    act.wait_ge(s_sum2, p)
                relu_twice(x2, acc1[par], s_x2)

            def relu3(p, last=False):
                act.wait_ge(s_used, step_no(p, STEPS - 1, last) + 1)
                if not (isinstance(p, int) and p == 0):
                    act.wait_ge(s_sum3, p)
                for c in range(2):
                    done = nc.scalar.activation(x3[:, c * HALF:(c + 1) * HALF], acc2[c * HID:(c + 1) * HID, :], ACT.Relu)
                done.then_inc(s_x3, 1)

            def tower_step(i, stage):
                act.wait_ge(s_tower, i * 4 + stage + 1)
                if stage == 0:
                    done = nc.scalar.activation(zb[HID:HID + CTX, :], tower[0:CTX, 0:BT], ACT.Copy)
                if stage == 1:
                    for m in range(TOP1 // P):
                        done = nc.scalar.activation(h1[:, m, :], tower[:, m * P:(m + 1) * P], ACT.Relu, bias=b1[:, m:m + 1])
                if stage == 2:
                    for m in range(TOP2 // P):
                        done = nc.scalar.activation(h2[:, m, :], tower[:, m * P:(m + 1) * P], ACT.Relu, bias=b2[:, m:m + 1])
                if stage == 3:
                    done = nc.scalar.activation(yv[:, :], tower[0:1, 0:BT], ACT.Copy)
                done.then_inc(s_act, 1)

            def period(i, par, first=False, last=False):
                p = i * PAR + par
                sum0_at = FIRST_SUM0_AT if first else SUM0_AT
                for s in range(STEPS):
                    if s == 0 and not first:
                        relu3(p - 1)
                    if s == N0 - 1:
                        relu2(p, par)
                    for kind, k, up in jobs_of(p if isinstance(p, int) else None, s):
                        job(kind, k, p + up, (par + up) % 2)
                    if sum0_at.get(s) == ROTS - 1 and not last:
                        relu1(p + 1, 1 - par)
                    if par == 0 and not first and s in TOWER_AT:
                        tower_step(i - 1, TOWER_AT[s])

            for kind, k, p in PROLOGUE:
                job(kind, k, p, p)
            relu1(0, 0)
            for kind, k, p in LATER:
                job(kind, k, p, p)
            act.wait_ge(s_top, 6 * 16)
            period(0, 0, first=True)
            period(0, 1)
            with act.Fori(1, TILES - 1) as i:
                period(i, 0)
                period(i, 1)
            period(TILES - 1, 0)
            period(TILES - 1, 1, last=True)
            relu3(TILES * PAR - 1, last=True)
            for stage in range(4):
                tower_step(TILES - 1, stage)


def kernel(**inputs):
    import numpy as np
    import concourse.bacc as bacc
    from concourse.bass_utils import run_bass_kernel_spmd

    nc = bacc.Bacc("TRN2", target_bir_lowering=False, num_devices=1)
    arrays, aps = {}, {}
    for name, value in inputs.items():
        a = np.ascontiguousarray(value)
        arrays[f"in_{name}"] = a
        aps[name] = nc.dram_tensor(f"in_{name}", a.shape, mybir.dt.from_np(a.dtype), kind="ExternalInput").ap()
    batch, fields = inputs["ids"].shape
    y = nc.dram_tensor("out_y", (batch, 1), mybir.dt.float32, kind="ExternalOutput").ap()
    cin_tower_kernel(nc, aps["dense_ctx"], aps["ids"], [aps[f"tbl_{f}"] for f in range(fields)],
                     aps["W_top1"], aps["b_top1"], aps["W_top2"], aps["b_top2"], aps["W_top3"],
                     aps["L0_rec_W0"], aps["L0_rec_W1"], aps["L0_rec_W2"], y)
    return run_bass_kernel_spmd(nc, [arrays], core_ids=[0]).results[0]["out_y"]
```

```python
import concourse.bass as bass
from concourse import mybir
from contextlib import ExitStack


def cin_tower_kernel(nc, dense_ctx, ids, tables, w_top1, b_top1, w_top2, b_top2, w_top3,
                     w_cin0, w_cin1, w_cin2, y_out):
    fp32, bf16, i32 = mybir.dt.float32, mybir.dt.bfloat16, mybir.dt.int32
    ALU, ACT = mybir.AluOpType, mybir.ActivationFunctionType

    P = 128
    BATCH, FIELDS = ids.shape
    EMB = tables[0].shape[1]
    HID = w_cin1.shape[2]
    CTX = dense_ctx.shape[1]
    TOP1, TOP2 = w_top1.shape[1], w_top2.shape[1]

    BT = P
    TILES = BATCH // BT
    PAR = 2
    HALF = 512
    N = 2 * HALF
    ND = N // BT
    PARTS = 3
    SK = PARTS * FIELDS

    ROWS = FIELDS * HID // P
    ROTS = 5
    RQ = P // FIELDS
    NROT = ROTS * RQ
    SYM = FIELDS - NROT

    DOUBLE = 12
    GROUPS = [(0, 4), (4, 4), (8, 4), (12, 2), (14, 2)]

    AHEAD = 4
    N0, C0 = ROWS - AHEAD, ROWS
    STEPS = 2 * ROWS
    RING = 4

    JOBS = [[] for _ in range(STEPS)]
    JOBS[C0 + 1].append(("stack", 0, 2))
    ROT_AT = (C0 + 3, C0 + 7, C0 + 10, C0 + 13, STEPS)
    for k, at in enumerate(ROT_AT):
        JOBS[at % STEPS].append(("rot", k, 2 - at // STEPS))
    SUM0 = [[] for _ in range(STEPS)]
    SUM0_AT = (C0 + 6, C0 + 9, C0 + 12, C0 + 15, STEPS + 3)
    for k, at in enumerate(SUM0_AT):
        SUM0[at % STEPS].append((k, 2 - at // STEPS))
    PROLOGUE = [("stack", 0, 0)] + [("rot", k, 0) for k in range(ROTS)]
    SHARED = PROLOGUE[0:2]
    LATER = [("stack", 0, 1), ("rot", 0, 1)]
    FIRST_JOBS = [[job for job in found if job[2] == 2] for found in JOBS]
    FIRST_SUM0 = [[(k, up) for k, up in found if up == 2] for found in SUM0]
    for k in range(ROTS):
        if k > 0:
            FIRST_JOBS[k].append(("rot", k, 1))
        FIRST_SUM0[2 + k].append((k, 1))

    EARLY = 29

    TOWER_AT = {6: 0, 9: 1, 12: 2, 15: 3}
    PERIODS = TILES * PAR

    def jobs_of(p, s):
        found = FIRST_JOBS[s] if p == 0 else JOBS[s]
        return [(kind, k, up) for kind, k, up in found if p is None or p + up < PERIODS]

    def sums_of(p, s):
        found = FIRST_SUM0[s] if p == 0 else SUM0[s]
        return [(k, up) for k, up in found if p is None or p + up < PERIODS]

    NUMBER = {}
    for kind, k, p in PROLOGUE + LATER:
        NUMBER[kind, k, p] = len(NUMBER)
    for p in range(PERIODS):
        for s in range(STEPS):
            for kind, k, up in jobs_of(p, s):
                NUMBER[kind, k, p + up] = len(NUMBER)
    PER_PERIOD = sum(len(x) for x in JOBS)

    def job_no(kind, k, p):
        return NUMBER[kind, k, p] if isinstance(p, int) else NUMBER[kind, k, 4] + (p - 4) * PER_PERIOD

    def job_buffer(kind, k, par, p):
        return job_no(kind, k, p if isinstance(p, int) else 4 + par) % 2

    def step_no(p, s, last=False):
        return p * STEPS + AHEAD + s - (AHEAD if last and s >= C0 else 0)

    HELP = [(PERIODS - 2, 2, 8), (PERIODS - 2, 2, 13),
            (PERIODS - 1, 1, 6), (PERIODS - 1, 1, 11),
            (PERIODS - 1, 2, 5), (PERIODS - 1, 2, 9), (PERIODS - 1, 2, 13)]
    HELP_STEPS = [step_no(p, t - AHEAD if layer == 1 else C0 + t, p == PERIODS - 1) for p, layer, t in HELP]

    def slot(par, t):
        return par * DOUBLE + t if t < DOUBLE else DOUBLE + t

    def gathered(n):
        return (n * FIELDS - EARLY) * 16

    def wait_for(eng, sem, value):
        if isinstance(value, int) and value <= 0:
            return
        eng.wait_ge(sem, value)

    def helped(n):
        return sum(step <= n for step in HELP_STEPS) if isinstance(n, int) else 0

    with ExitStack() as ctx:
        def sb(name, shape, dt=fp32):
            return ctx.enter_context(nc.sbuf_tensor(name, shape, dt))

        def sem(name):
            return ctx.enter_context(nc.semaphore(name))

        w0 = sb("w0", [P, ROTS, HID])
        w1 = sb("w1", [P, ROWS, HID])
        w2 = sb("w2", [P, ROWS, HID])
        t1a = sb("t1a", [P, TOP1])
        t1b = sb("t1b", [HID + CTX, TOP1])
        t2 = sb("t2", [P, TOP1 // P, TOP2])
        t3 = sb("t3", [P, TOP2 // P])
        b1 = sb("b1", [P, TOP1 // P])
        b2 = sb("b2", [P, TOP2 // P])
        ident = sb("ident", [P, P])
        ident_h = sb("ident_h", [P, P], bf16)
        fold = sb("fold", [SK, FIELDS])
        unit = sb("unit", [SK, 2 * FIELDS], bf16)
        sel_rot = sb("sel_rot", [SK, ROTS, P], bf16)
        row_col = sb("row_col", [FIELDS, 2, HID])
        idx = sb("idx", [P, FIELDS], i32)
        emb = sb("emb", [P, FIELDS * EMB])
        zero = sb("zero", [P, 1])
        parts = sb("parts", [P, PARTS, FIELDS * EMB], bf16)
        dense = sb("dense", [P, CTX])
        stack = [sb(f"stack{n}", [SK, N], bf16) for n in range(2)]
        x3_field = sb("x3_field", [HID + FIELDS, N])
        x3, field = x3_field[0:HID, :], x3_field[HID:HID + FIELDS, :]
        rows = sb("rows", [P, DOUBLE + ROWS, N])
        squares = sb("squares", [P, ROTS, N])
        prod = sb("prod", [P, RING, N])
        x1 = [sb(f"x1{n}", [P, N]) for n in "ab"]
        x2 = sb("x2", [P, N])
        tmp = sb("tmp", [P, HALF + HALF // 2])
        rest = tmp[:, 0:FIELDS * EMB]
        half_sum = sb("half_sum", [P, 3, BT])
        za = sb("za", [P, BT])
        zb = sb("zb", [HID + CTX, BT])
        h1 = sb("h1", [P, TOP1 // P, BT])
        w0_mirror = h1[:, :, :].rearrange("p m b -> p (m b)")[:, 0:ROTS * HID]
        w0_mirror = w0_mirror.rearrange("p (t k) -> p t k", k=HID)
        h2 = sb("h2", [P, TOP2 // P, BT])
        yv = sb("yv", [1, BT])

        spread = [ctx.enter_context(nc.psum_tensor(f"spread{i}", [P, N], fp32)) for i in range(2)]
        acc0 = ctx.enter_context(nc.psum_tensor("acc0", [P, HALF], fp32))
        acc1 = [ctx.enter_context(nc.psum_tensor(f"acc1{n}", [P, HALF], fp32)) for n in "ab"]
        acc2 = ctx.enter_context(nc.psum_tensor("acc2", [P, HALF], fp32))
        tower = acc0

        w0_wide = nc.dram_tensor("w0_wide", [FIELDS, 2 * FIELDS, HID], fp32, kind="Internal").ap()
        w0_tall = nc.dram_tensor("w0_tall", [2 * FIELDS, FIELDS, HID], fp32, kind="Internal").ap()

        field_dram = nc.dram_tensor("field_dram", [2, FIELDS, N], fp32, kind="Internal").ap()

        s_wide = sem("s_wide")
        s_w0 = sem("s_w0")
        s_w12 = sem("s_w12")
        s_top = sem("s_top")
        s_idx = sem("s_idx")
        s_dense = sem("s_dense")
        s_ident0 = sem("s_ident0")
        s_ident = sem("s_ident")
        s_const = sem("s_const")
        s_sel = sem("s_sel")
        s_w0sum = sem("s_w0sum")
        s_early = sem("s_early")
        s_gather = sem("s_gather")
        s_first_split = sem("s_first_split")
        s_split = sem("s_split")
        s_add = [sem(f"s_add{n}") for n in range(1, 4)]
        s_parts = sem("s_parts")
        s_spread = sem("s_spread")
        s_copied = sem("s_copied")
        s_taken = sem("s_taken")
        s_prod = sem("s_prod")
        s_helped = sem("s_helped")
        s_halved = sem("s_halved")
        s_field = sem("s_field")
        s_rows = [sem(f"s_rows{g}") for g in range(len(GROUPS))]
        s_first = [sem(f"s_first{t}") for t in range(GROUPS[0][1])]
        s_sum0 = sem("s_sum0")
        s_w0loads = sem("s_w0loads")
        s_used = sem("s_used")
        s_x1 = sem("s_x1")
        s_x2 = sem("s_x2")
        s_x3 = sem("s_x3")
        s_sum1 = sem("s_sum1")
        s_sum2 = sem("s_sum2")
        s_sum3 = sem("s_sum3")
        s_last = sem("s_last")
        s_tower = sem("s_tower")
        s_act = sem("s_act")
        s_y = sem("s_y")

        def wait_products(eng, n):
            eng.wait_ge(s_prod, n + 1 - helped(n))
            wait_for(eng, s_helped, helped(n))

        block = ctx.enter_context(nc.Block())

        @block.sync
        def _(sp):
            def load_tile(i):
                if not (isinstance(i, int) and i == 0):
                    sp.wait_ge(s_gather, gathered(i))
                sp.dma_start(idx[:, :], ids[bass.ts(i, BT), :]).then_inc(s_idx, 16)

            def load_dense(i):
                sp.dma_start(dense[:, :], dense_ctx[bass.ts(i, BT), :]).then_inc(s_dense, 16)

            def store(i):
                sp.wait_ge(s_act, (i + 1) * 4)
                sp.dma_start(y_out[bass.ts(i, BT), :].rearrange("b o -> o b"), yv[:, :]).then_inc(s_y, 16)
                sp.wait_ge(s_y, (i + 1) * 16)

            def field_out(p, par):
                sp.wait_ge(s_halved, p + 1)
                if isinstance(p, int) and p == 0:
                    sp.wait_ge(s_taken, 2)
                sp.dma_start(field_dram[par, :, :], field[:, :]).then_inc(s_field, 16)
                sp.wait_ge(s_field, (p + 1) * 16)

            def spread_rows(par, t, count, done):
                for c in range(2):
                    src = bass.AP(field_dram.tensor, (par * FIELDS + 2 * t + c) * N,
                                  [[0, HID], [2 * N, count], [1, N]])
                    at = slot(par, t)
                    sp.dma_start(rows[c * HID:(c + 1) * HID, at:at + count, :], src).then_inc(done, 16)

            def rows_in(p, par, groups):
                for g in groups:
                    t, count = GROUPS[g]
                    if t >= DOUBLE and not (isinstance(p, int) and p == 0):
                        wait_products(sp, step_no(p - 1, C0 + t + count - 1))
                    spread_rows(par, t, count, s_rows[g])

            load_tile(0)
            sp.dma_start(prod[0:FIELDS, 0:2, :].rearrange("a x y -> a (x y)"),
                         w_cin0.rearrange("a b k -> a (b k)")).then_inc(s_w0loads, 16)
            sp.dma_start(prod[0:FIELDS, 2:4, :].rearrange("b x y -> b (x y)").rearrange("b (a k) -> b a k", k=HID),
                         w_cin0.rearrange("a b k -> b a k")).then_inc(s_w0loads, 16)
            for c in range(2):
                sp.dma_start(w0_wide[:, c * FIELDS:(c + 1) * FIELDS, :], w_cin0).then_inc(s_wide, 16)
                sp.dma_start(w0_tall[c * FIELDS:(c + 1) * FIELDS, :, :], w_cin0).then_inc(s_wide, 16)
            load_dense(0)
            sp.dma_start(w1[:, :, :], w_cin1.rearrange("m h k -> (m h) k")
                         .rearrange("(t p) k -> p t k", p=P)).then_inc(s_w12, 16)
            sp.dma_start(w2[:, :, :], w_cin2.rearrange("m h k -> (m h) k")
                         .rearrange("(t p) k -> p t k", p=P)).then_inc(s_w12, 16)
            sp.wait_ge(s_wide, 64)
            for q in range(RQ):
                at = slice(q * FIELDS, (q + 1) * FIELDS)
                sp.dma_start(w0[at, :, :], bass.AP(w0_wide.tensor, q * HID, [
                    [(2 * FIELDS + 1) * HID, FIELDS], [RQ * HID, ROTS], [1, HID]])).then_inc(s_w0, 16)
                sp.dma_start(w0_mirror[at, :, :], bass.AP(w0_tall.tensor, q * FIELDS * HID, [
                    [(FIELDS + 1) * HID, FIELDS], [RQ * FIELDS * HID, ROTS], [1, HID]])).then_inc(s_w0, 16)
            sp.dma_start(t1a[:, :], w_top1[0:P, :]).then_inc(s_top, 16)
            sp.dma_start(t1b[:, :], w_top1[P:, :]).then_inc(s_top, 16)
            sp.dma_start(t2[:, :, :], w_top2.rearrange("(t p) n -> p t n", p=P)).then_inc(s_top, 16)
            sp.dma_start(t3[:, :], w_top3.rearrange("(t p) o -> p (t o)", p=P),
                         allow_slow_non_contiguous=True).then_inc(s_top, 16)
            sp.dma_start(b1[:, :], b_top1.rearrange("(t p) -> p t", p=P),
                         allow_slow_non_contiguous=True).then_inc(s_top, 16)
            sp.dma_start(b2[:, :], b_top2.rearrange("(t p) -> p t", p=P),
                         allow_slow_non_contiguous=True).then_inc(s_top, 16)
            load_tile(1)
            field_out(0, 0)
            for t in range(GROUPS[0][1]):
                spread_rows(0, t, 1, s_first[t])
            rows_in(0, 0, (1, 2, 3, 4))
            field_out(1, 1)
            rows_in(1, 1, (0, 1, 2))

            def ahead(p, par, last=False, tile=None):
                if not last:
                    field_out(p + 2, par)
                    rows_in(p + 2, par, (0,))
                rows_in(p + 1, 1 - par, (3, 4))
                if tile is not None:
                    load_tile(tile)
                if not last:
                    rows_in(p + 2, par, (1, 2))

            def turn(i, ids_too=True, first=False, last=False):
                ahead(i * PAR, 0, last)
                if not first:
                    store(i - 1)
                    load_dense(i)
                if not last:
                    ahead(i * PAR + 1, 1, tile=i + 3 if ids_too else None)

            load_tile(2)
            turn(0, first=True)
            with sp.Fori(1, TILES - 3) as i:
                turn(i)
            turn(TILES - 3, ids_too=False)
            turn(TILES - 2, ids_too=False)
            turn(TILES - 1, ids_too=False, last=True)
            store(TILES - 1)

        @block.gpsimd
        def _(pool):
            nc.gpsimd.memset(zero[:, :], 0.0).then_inc(s_ident0, 1)
            zeros = zero[:, :].to_broadcast([P, FIELDS * EMB])
            nc.gpsimd.memset(ident[:, :], 0.0).then_inc(s_ident0, 1)
            pool.wait_ge(s_ident0, 2)
            nc.gpsimd.affine_select(out=ident[:, :], in_=ident[:, :], compare_op=ALU.not_equal, fill=1.0,
                                    base=0, pattern=[[-1, P]], channel_multiplier=1).then_inc(s_ident, 1)

            def gather(i, fields):
                pool.drain()
                for f in fields:
                    pool.indirect_dma_start(
                        out=emb[:, f * EMB:(f + 1) * EMB], out_offset=None, in_=tables[f],
                        in_offset=bass.IndirectOffsetOnAxis(ap=idx[:, f:f + 1], axis=0)
                    ).then_inc(s_early if isinstance(i, int) and i == 0 and f < EARLY else s_gather, 16)

            def split(i):
                pool.drain()
                pool.wait_ge(s_gather, gathered(i + 1))
                pool.wait_ge(s_spread, job_no("stack", 0, (i - 1) * PAR + 1) + 1)
                nc.gpsimd.tensor_tensor(parts[:, 0, :], emb[:, :], zeros, ALU.add).then_inc(s_split, 1)
                pool.wait_ge(s_split, (i - 1) * 3 + 1)
                nc.gpsimd.tensor_tensor(rest[:, :], emb[:, :], parts[:, 0, :], ALU.subtract).then_inc(s_split, 1)
                pool.wait_ge(s_split, (i - 1) * 3 + 2)
                nc.gpsimd.tensor_tensor(parts[:, 1, :], rest[:, :], zeros, ALU.add).then_inc(s_split, 1)
                pool.wait_ge(s_split, (i - 1) * 3 + 3)
                nc.gpsimd.tensor_tensor(parts[:, 2, :], rest[:, :], parts[:, 1, :], ALU.subtract).then_inc(s_parts, 1)

            def sum_d(x, lo, layer, i, par, out, done):
                r = slice(lo, lo + HID)
                q = HALF // 2
                add, base = s_add[layer], i * 5 + 2 * par
                nc.gpsimd.tensor_tensor(tmp[r, 0:HALF], x[r, 0:HALF], x[r, HALF:N], ALU.add).then_inc(add, 1)
                pool.wait_ge(add, base + 1)
                nc.gpsimd.tensor_tensor(tmp[r, HALF:HALF + q], tmp[r, 0:q], tmp[r, q:HALF], ALU.add).then_inc(add, 1)
                pool.wait_ge(add, base + 2)
                a, b = tmp[r, HALF:HALF + BT], tmp[r, HALF + BT:HALF + q]
                if par == 0:
                    nc.gpsimd.tensor_tensor(half_sum[r, layer, :], a, b, ALU.add).then_inc(done, 1)
                else:
                    nc.gpsimd.tensor_tensor(tmp[r, 0:BT], a, b, ALU.add).then_inc(add, 1)
                    pool.wait_ge(add, base + 3)
                    nc.gpsimd.tensor_tensor(out, tmp[r, 0:BT], half_sum[r, layer, :], ALU.add).then_inc(done, 1)

            def sum1(i, par):
                pool.drain()
                pool.wait_ge(s_x1, i * PAR + par + 1)
                sum_d(x1[par], 0, 0, i, par, za[0:HID, :], s_sum1)

            def sum2(i, par, ids_of=None):
                pool.drain()
                if ids_of is not None:
                    pool.wait_ge(s_idx, (ids_of + 1) * 16)
                pool.wait_ge(s_x2, i * PAR + par + 1)
                sum_d(x2, HID, 1, i, par, za[HID:P, :], s_sum2)

            def sum3(i, par):
                pool.drain()
                pool.wait_ge(s_x3, i * PAR + par + 1)
                sum_d(x3, 0, 2, i, par, zb[0:HID, :], s_sum3)

            def help_out(k):
                p, layer, t = HELP[k]
                x = x1[p % PAR] if layer == 1 else x2
                pool.drain()
                if layer == 1:
                    g = [t >= start for start, _ in GROUPS].count(True) - 1
                    pool.wait_ge(s_rows[g], (p + 1) * 32)
                    pool.wait_ge(s_x1, p + 1)
                else:
                    pool.wait_ge(s_x2, p + 1)
                pool.wait_ge(s_used, HELP_STEPS[k] - RING + 1)
                nc.gpsimd.tensor_tensor(prod[:, t % RING, :], rows[:, slot(p % PAR, t), :], x[:, :],
                                        ALU.mult).then_inc(s_helped, 1)

            def turn(i, more=True, last=False):
                sum3(i - 1, 1)
                if not last:
                    split(i + 1)
                sum1(i, 0)
                rest_of_turn(i, more, last)

            def rest_of_turn(i, more=True, last=False):
                if more:
                    sum2(i, 0, ids_of=i + 2)
                    gather(i + 2, range(0, FIELDS // 2))
                else:
                    sum2(i, 0)
                if last:
                    sum1(i, 1)
                    for k in range(3):
                        help_out(k)
                    sum3(i, 0)
                    help_out(3)
                else:
                    sum3(i, 0)
                    sum1(i, 1)
                if more:
                    gather(i + 2, range(FIELDS // 2, FIELDS))
                sum2(i, 1)
                if last:
                    for k in range(4, len(HELP)):
                        help_out(k)

            pool.wait_ge(s_idx, 16)
            gather(0, range(FIELDS))
            pool.wait_ge(s_idx, 32)
            pool.wait_ge(s_parts, 1)
            gather(1, range(FIELDS))
            sum1(0, 0)
            split(1)
            rest_of_turn(0)
            with pool.Fori(1, TILES - 2) as i:
                turn(i)
            turn(TILES - 2, more=False)
            turn(TILES - 1, more=False, last=True)

        @block.vector
        def _(dve):
            dve.wait_ge(s_ident, 1)
            nc.vector.tensor_copy(ident_h[:, :], ident[:, :])
            nc.vector.tensor_tensor(fold[:, :], ident[0:SK, 0:FIELDS], ident[0:SK, FIELDS:2 * FIELDS],
                                    ALU.add).then_inc(s_const, 1)
            dve.wait_ge(s_const, 1)
            for c in range(2):
                nc.vector.tensor_tensor(unit[:, c * FIELDS:(c + 1) * FIELDS], fold[:, :],
                                        ident[0:SK, 2 * FIELDS:3 * FIELDS], ALU.add).then_inc(s_const, 1)
            dve.wait_ge(s_const, 3)
            for j in range(NROT):
                nc.vector.tensor_tensor(sel_rot[:, j // RQ, (j % RQ) * FIELDS:(j % RQ + 1) * FIELDS],
                                        unit[:, 0:FIELDS], unit[:, j:j + FIELDS], ALU.add).then_inc(s_sel, 1)
            dve.wait_ge(s_w0, 2 * RQ * 16)
            for q in range(RQ):
                at = slice(q * FIELDS, (q + 1) * FIELDS)
                ts = [t for t in range(ROTS) if 1 <= t * RQ + q <= SYM]
                span = slice(ts[0], ts[-1] + 1)
                last = nc.vector.tensor_tensor(w0[at, span, :], w0[at, span, :], w0_mirror[at, span, :], ALU.add)
            last.then_inc(s_const, 1)
            dve.wait_ge(s_w0loads, 32)
            for c in range(2):
                nc.vector.tensor_reduce(row_col[:, c, :], prod[0:FIELDS, 2 * c:2 * c + 2, :]
                                        .rearrange("a x y -> a (x y)").rearrange("a (b k) -> a k b", k=HID),
                                        mybir.AxisListType.X, ALU.add).then_inc(s_const, 1)
            dve.wait_ge(s_const, 6)
            nc.vector.tensor_scalar(w0[:, :, :], w0[:, :, :], 0.5, None, ALU.mult).then_inc(s_const, 1)
            nc.vector.tensor_tensor(row_col[:, 0, :], row_col[:, 0, :], row_col[:, 1, :], ALU.add).then_inc(s_const, 1)
            dve.wait_ge(s_const, 8)
            nc.vector.scalar_tensor_tensor(out=w0[0:FIELDS, 0, :], in0=row_col[:, 0, :], scalar=-0.125,
                                           in1=w0[0:FIELDS, 0, :], op0=ALU.mult, op1=ALU.add).then_inc(s_w0sum, 1)

            def outer(p, par, layer, t, n):
                if layer == 1:
                    if isinstance(p, int) and p == 0 and t < GROUPS[0][1]:
                        dve.wait_ge(s_first[t], 32)
                    else:
                        for g, (start, _) in enumerate(GROUPS):
                            if t == start:
                                dve.wait_ge(s_rows[g], (p + 1 if g > 0 else p) * 32)
                if layer == 1 and t == 0:
                    dve.wait_ge(s_x1, p + 1)
                if layer == 2 and t == 0:
                    dve.wait_ge(s_x2, p + 1)
                if isinstance(n, int) and n in HELP_STEPS:
                    return
                wait_for(dve, s_used, n - RING + 1)
                nc.vector.tensor_tensor(prod[:, t % RING, :], rows[:, slot(par, t), :],
                                        x1[par][:, :] if layer == 1 else x2[:, :], ALU.mult).then_inc(s_prod, 1)

            def period(i, par, last=False):
                p = i * PAR + par
                for t in range(AHEAD, ROWS):
                    outer(p, par, 1, t, step_no(p, t - AHEAD))
                if not last:
                    for t in range(AHEAD):
                        outer(p + 1, 1 - par, 1, t, step_no(p, N0 + t))
                for t in range(ROWS):
                    outer(p, par, 2, t, step_no(p, C0 + t, last))

            dve.wait_ge(s_early, EARLY * 16)
            for step, cols in enumerate((slice(0, EARLY * EMB), slice(EARLY * EMB, FIELDS * EMB))):
                if step == 1:
                    dve.wait_ge(s_gather, gathered(1))
                left = x2[:, cols]
                nc.vector.tensor_copy(parts[:, 0, cols], emb[:, cols]).then_inc(s_first_split, 1)
                dve.wait_ge(s_first_split, step * 3 + 1)
                nc.vector.tensor_tensor(left, emb[:, cols], parts[:, 0, cols], ALU.subtract).then_inc(s_first_split, 1)
                dve.wait_ge(s_first_split, step * 3 + 2)
                nc.vector.tensor_copy(parts[:, 1, cols], left).then_inc(s_first_split, 1)
                dve.wait_ge(s_first_split, step * 3 + 3)
                last = nc.vector.tensor_tensor(parts[:, 2, cols], left, parts[:, 1, cols], ALU.subtract)
            last.then_inc(s_parts, 1)
            for n, (kind, k, p) in enumerate(SHARED):
                got, cols = spread[n % 2], slice(HALF, N)
                dve.wait_ge(s_spread, n + 1)
                if kind == "stack":
                    done = nc.vector.tensor_copy(stack[p][:, cols], got[0:SK, cols])
                else:
                    done = nc.vector.tensor_scalar(field[:, cols], got[0:FIELDS, cols], 0.5, None, ALU.mult)
                done.then_inc(s_taken, 1)

            for t in range(AHEAD):
                outer(0, 0, 1, t, t)
            period(0, 0)
            period(0, 1)
            with dve.Fori(1, TILES - 1) as i:
                period(i, 0)
                period(i, 1)
            period(TILES - 1, 0)
            period(TILES - 1, 1, last=True)
            last_sum = squares[0:HID, 0, 0:BT]
            dve.wait_ge(s_x3, PERIODS)
            nc.vector.tensor_reduce(last_sum, x3.rearrange("k (d b) -> k b d", b=BT),
                                    mybir.AxisListType.X, ALU.add).then_inc(s_last, 1)
            dve.wait_ge(s_last, 1)
            dve.wait_ge(s_sum3, PERIODS - 1)
            nc.vector.tensor_tensor(zb[0:HID, :], last_sum, half_sum[0:HID, 2, :], ALU.add).then_inc(s_sum3, 1)

        @block.tensor
        def _(pe):
            def job(kind, k, p, par):
                n = job_no(kind, k, p)
                taken = job_no("stack", 0, p) + 1 if (kind, k) == ("rot", 0) else n - 1
                wait_for(pe, s_copied, taken)
                if isinstance(p, int) and (kind, k, p) in PROLOGUE + LATER:
                    wait_for(pe, s_taken, min(taken, len(SHARED)))
                out = spread[job_buffer(kind, k, par, p)]
                if kind == "stack":
                    lhs = parts[:, :, :].rearrange("b s (m d) -> b s m d", d=EMB)
                    for d in range(ND):
                        last = nc.tensor.matmul(out[0:SK, d * BT:(d + 1) * BT], lhs[:, :, :, par * ND + d],
                                                ident_h[:, :], start=True, stop=True)
                else:
                    for c in range(2):
                        cols = slice(c * HALF, (c + 1) * HALF)
                        last = nc.tensor.matmul(out[:, cols], sel_rot[:, k, :], stack[par][:, cols],
                                                start=True, stop=True)
                last.then_inc(s_spread, 1)

            def contract(acc, w, operand, first, last):
                for c in range(2):
                    mm = nc.tensor.matmul(acc[c * HID:(c + 1) * HID, :], w, operand[:, c * HALF:(c + 1) * HALF],
                                          start=first, stop=last)
                return mm

            def layer0(k, p):
                pe.wait_ge(s_copied, job_no("rot", k, p) + 1)
                mm = contract(acc0, w0[:, k, :], squares[:, k, :], k == 0, k == ROTS - 1)
                if k == ROTS - 1:
                    mm.then_inc(s_sum0, 1)

            def outer(w, t, acc, n):
                wait_products(pe, n)
                contract(acc, w[:, t, :], prod[:, t % RING, :], t == 0, t == ROWS - 1).then_inc(s_used, 1)

            def tower_step(i, stage):
                if stage == 0:
                    pe.wait_ge(s_dense, (i + 1) * 16)
                    pe.wait_ge(s_x1, PERIODS if isinstance(i, int) and i == TILES - 1 else (i + 2) * PAR)
                    mm = nc.tensor.matmul(tower[0:CTX, 0:BT], dense[:, :], ident[:, :], start=True, stop=True)
                else:
                    pe.wait_ge(s_act, i * 4 + stage)
                if stage == 1:
                    pe.wait_ge(s_sum1, (i + 1) * PAR)
                    pe.wait_ge(s_sum2, (i + 1) * PAR)
                    pe.wait_ge(s_sum3, (i + 1) * PAR)
                    for m in range(TOP1 // P):
                        cols = slice(m * P, (m + 1) * P)
                        nc.tensor.matmul(tower[:, cols], t1a[:, cols], za[:, :], start=True, stop=False)
                        mm = nc.tensor.matmul(tower[:, cols], t1b[:, cols], zb[:, :], start=False, stop=True)
                if stage == 2:
                    for m in range(TOP2 // P):
                        cols = slice(m * P, (m + 1) * P)
                        for k in range(TOP1 // P):
                            mm = nc.tensor.matmul(tower[:, cols], t2[:, k, cols], h1[:, k, :],
                                                  start=(k == 0), stop=(k == TOP1 // P - 1))
                if stage == 3:
                    for k in range(TOP2 // P):
                        mm = nc.tensor.matmul(tower[0:1, 0:BT], t3[:, k:k + 1], h2[:, k, :],
                                              start=(k == 0), stop=(k == TOP2 // P - 1))
                mm.then_inc(s_tower, 1)

            def period(i, par, first=False, last=False):
                p = i * PAR + par
                for s in range(STEPS):
                    if s < N0:
                        outer(w1, s + AHEAD, acc1[par], step_no(p, s))
                    elif s < C0:
                        if s == N0:
                            wait_for(pe, s_x2, p)
                        if not last:
                            outer(w1, s - N0, acc1[1 - par], step_no(p, s))
                    else:
                        if s == C0:
                            wait_for(pe, s_x3, p)
                        outer(w2, s - C0, acc2, step_no(p, s, last))
                    for kind, k, up in jobs_of(p if isinstance(p, int) else None, s):
                        if kind == "stack" and par == 0 and up == PAR:
                            pe.wait_ge(s_parts, i + 2)
                        job(kind, k, p + up, (par + up) % 2)
                    for k, up in sums_of(p if isinstance(p, int) else None, s):
                        if k == 0:
                            pe.wait_ge(s_x1, p + up)
                            if par == 0 and not first:
                                pe.wait_ge(s_act, i * 4)
                        layer0(k, p + up)
                    if par == 0 and not first and s in TOWER_AT:
                        tower_step(i - 1, TOWER_AT[s])

            pe.wait_ge(s_sel, NROT)
            pe.wait_ge(s_parts, 1)
            for kind, k, p in PROLOGUE:
                job(kind, k, p, p)
                if kind == "rot" and k == 2:
                    pe.wait_ge(s_w0sum, 1)
                if kind == "rot" and k >= 2:
                    layer0(k - 2, 0)
            for k in range(ROTS - 2, ROTS):
                layer0(k, 0)
            for kind, k, p in LATER:
                job(kind, k, p, p)
            pe.wait_ge(s_w12, 32)
            pe.wait_ge(s_top, 6 * 16)
            for t in range(AHEAD):
                outer(w1, t, acc1[0], t)
            period(0, 0, first=True)
            period(0, 1)
            with pe.Fori(1, TILES - 1) as i:
                period(i, 0)
                period(i, 1)
            period(TILES - 1, 0)
            period(TILES - 1, 1, last=True)
            for stage in range(4):
                tower_step(TILES - 1, stage)

        @block.scalar
        def _(act):
            def job(kind, k, p, par):
                n = job_no(kind, k, p)
                got = spread[job_buffer(kind, k, par, p)]
                act.wait_ge(s_spread, n + 1)
                shared = isinstance(p, int) and (kind, k, p) in SHARED
                cols = slice(0, HALF if shared else N)
                if kind == "stack":
                    done = nc.scalar.activation(stack[par][:, cols], got[0:SK, cols], ACT.Copy)
                else:
                    if k == 0:
                        if not (isinstance(p, int) and p == 0):
                            act.wait_ge(s_field, p * 16)
                        nc.scalar.activation(field[:, cols], got[0:FIELDS, cols], ACT.Copy,
                                             scale=0.5).then_inc(s_halved, 1)
                        if shared:
                            act.wait_ge(s_taken, len(SHARED))
                    wait_for(act, s_sum0, p)
                    done = nc.scalar.activation(squares[:, k, :], got[:, :], ACT.Square)
                done.then_inc(s_copied, 1)

            def relu_twice(x, acc, done):
                for c in range(2):
                    for h in range(2):
                        last = nc.scalar.activation(x[h * HID:(h + 1) * HID, c * HALF:(c + 1) * HALF],
                                                    acc[c * HID:(c + 1) * HID, :], ACT.Relu)
                last.then_inc(done, 1)

            def relu1(p, par):
                act.wait_ge(s_sum0, p + 1)
                if not (isinstance(p, int) and p < 2):
                    wait_products(act, step_no(p - 2, N0 - 1))
                    act.wait_ge(s_sum1, p - 1)
                relu_twice(x1[par], acc0, s_x1)

            def relu2(p, par):
                act.wait_ge(s_used, step_no(p, N0 - 1) + 1)
                if not (isinstance(p, int) and p == 0):
                    wait_products(act, step_no(p - 1, STEPS - 1))
                    act.wait_ge(s_sum2, p)
                relu_twice(x2, acc1[par], s_x2)

            def relu3(p, last=False):
                act.wait_ge(s_used, step_no(p, STEPS - 1, last) + 1)
                if not (isinstance(p, int) and p == 0):
                    act.wait_ge(s_sum3, p)
                for c in range(2):
                    done = nc.scalar.activation(x3[:, c * HALF:(c + 1) * HALF], acc2[c * HID:(c + 1) * HID, :], ACT.Relu)
                done.then_inc(s_x3, 1)

            def tower_step(i, stage):
                act.wait_ge(s_tower, i * 4 + stage + 1)
                if stage == 0:
                    done = nc.scalar.activation(zb[HID:HID + CTX, :], tower[0:CTX, 0:BT], ACT.Copy)
                if stage == 1:
                    for m in range(TOP1 // P):
                        done = nc.scalar.activation(h1[:, m, :], tower[:, m * P:(m + 1) * P], ACT.Relu, bias=b1[:, m:m + 1])
                if stage == 2:
                    for m in range(TOP2 // P):
                        done = nc.scalar.activation(h2[:, m, :], tower[:, m * P:(m + 1) * P], ACT.Relu, bias=b2[:, m:m + 1])
                if stage == 3:
                    done = nc.scalar.activation(yv[:, :], tower[0:1, 0:BT], ACT.Copy)
                done.then_inc(s_act, 1)

            def period(i, par, first=False, last=False):
                p = i * PAR + par
                for s in range(STEPS):
                    if s == 0 and not first:
                        relu3(p - 1)
                    if s == N0 - 1:
                        relu2(p, par)
                    for kind, k, up in jobs_of(p if isinstance(p, int) else None, s):
                        job(kind, k, p + up, (par + up) % 2)
                    for k, up in sums_of(p if isinstance(p, int) else None, s):
                        if k == ROTS - 1:
                            relu1(p + up, (par + up) % 2)
                    if par == 0 and not first and s in TOWER_AT:
                        tower_step(i - 1, TOWER_AT[s])

            for kind, k, p in PROLOGUE:
                job(kind, k, p, p)
            relu1(0, 0)
            for kind, k, p in LATER:
                job(kind, k, p, p)
            act.wait_ge(s_top, 6 * 16)
            period(0, 0, first=True)
            period(0, 1)
            with act.Fori(1, TILES - 1) as i:
                period(i, 0)
                period(i, 1)
            period(TILES - 1, 0)
            period(TILES - 1, 1, last=True)
            relu3(TILES * PAR - 1, last=True)
            for stage in range(4):
                tower_step(TILES - 1, stage)


def kernel(**inputs):
    import numpy as np
    import concourse.bacc as bacc
    from concourse.bass_utils import run_bass_kernel_spmd

    nc = bacc.Bacc("TRN2", target_bir_lowering=False, num_devices=1)
    arrays, aps = {}, {}
    for name, value in inputs.items():
        a = np.ascontiguousarray(value)
        arrays[f"in_{name}"] = a
        aps[name] = nc.dram_tensor(f"in_{name}", a.shape, mybir.dt.from_np(a.dtype), kind="ExternalInput").ap()
    batch, fields = inputs["ids"].shape
    y = nc.dram_tensor("out_y", (batch, 1), mybir.dt.float32, kind="ExternalOutput").ap()
    cin_tower_kernel(nc, aps["dense_ctx"], aps["ids"], [aps[f"tbl_{f}"] for f in range(fields)],
                     aps["W_top1"], aps["b_top1"], aps["W_top2"], aps["b_top2"], aps["W_top3"],
                     aps["L0_rec_W0"], aps["L0_rec_W1"], aps["L0_rec_W2"], y)
    return run_bass_kernel_spmd(nc, [arrays], core_ids=[0]).results[0]["out_y"]
```
